# Optimizing a Trainium2 kernel written in Bass

```python
import numpy as np
import jax
import jax.numpy as jnp

def _softmax(x, axis=-1):
    return jax.nn.softmax(x, axis=axis)
def _gelu(x):
    return jax.nn.gelu(x, approximate=True)
def _silu(x):
    return jax.nn.silu(x)
def _sigmoid(x):
    return jax.nn.sigmoid(x)
def _layernorm(x, axis=-1, eps=1e-5):
    m = jnp.mean(x, axis=axis, keepdims=True)
    v = jnp.var(x, axis=axis, keepdims=True)
    return (x - m) / jnp.sqrt(v + eps)
def _scatter_add(tgt, idx, src, axis=0):
    return tgt.at[idx].add(src)
def _segment_sum(src, seg, n):
    return jax.ops.segment_sum(src, seg, n)

kernel_name = 'mk_adj_resnorm_d2_adj_256_182b1b'

def setup_inputs(seed: int = 0):
    np.random.seed(seed)
    _w = jnp.asarray
    def _rec_inputs():
        import jax
        import jax.numpy as jnp
        _gk = jax.random.key(seed)
        x = -0.000929 + 1 * jax.random.normal(jax.random.fold_in(_gk, 1), (3327, 256), jnp.float32)
        _a = jax.random.bernoulli(jax.random.fold_in(_gk, 2), 0.00961827, (3327, 3327))
        _a = jnp.logical_or(_a, jnp.swapaxes(_a, -1, -2))
        _a = jnp.logical_or(_a, jnp.eye(3327, dtype=bool))
        _af = _a.astype(jnp.float32)
        _af = _af * jax.random.uniform(jax.random.fold_in(_gk, 3), (3327, 3327), jnp.float32, 0.05, 1)
        adj = _af
        return x, adj
    x, adj = _rec_inputs()
    def _L0_gnn_setup():
        import jax, jax.numpy as jnp
        import numpy as np
        N, H, HEADS = (4096, 256, 3)
        ALPHA = 0.2
        NEG_INF = -9000000000000000.0

        def _sign_adj(key, n, density):
            k1, k2 = jax.random.split(key)
            mask = jax.random.uniform(k1, (n, n)) < density
            sign = jnp.where(jax.random.uniform(k2, (n, n)) < 0.5, -1.0, 1.0)
            adj = jnp.where(mask, sign, 0.0).astype(jnp.float32)
            idx = jnp.arange(n)
            return adj.at[idx, idx].set(1.0)

        def _gru_cell(x, hstate, Wih, Whh, bih, bhh):
            gi = x @ Wih.T + bih
            gh = hstate @ Whh.T + bhh
            ir, iz, inn = jnp.split(gi, 3, axis=1)
            hr, hz, hn = jnp.split(gh, 3, axis=1)
            r = jax.nn.sigmoid(ir + hr)
            z = jax.nn.sigmoid(iz + hz)
            n = jnp.tanh(inn + r * hn)
            return (1.0 - z) * n + z * hstate

        def _gat_head(h, node_adj, edge_adj, W, a):
            hW = h @ W
            hp = (node_adj > 0).astype(hW.dtype) @ hW
            hm = (node_adj < 0).astype(hW.dtype) @ hW
            e_plus = jax.nn.leaky_relu(jnp.concatenate([hp, hm], axis=1) @ a, ALPHA)[:, 0]
            e_minus = jax.nn.leaky_relu(jnp.concatenate([hm, hp], axis=1) @ a, ALPHA)[:, 0]
            att = jnp.where(edge_adj > 0, e_plus[None, :], NEG_INF)
            att = jnp.where(edge_adj < 0, e_minus[None, :], att)
            att = jax.nn.softmax(att, axis=1)
            return att * edge_adj @ hW
        key = jax.random.key(seed)
        ks = jax.random.split(key, 16)
        std = 0.01
        gain = 1.414
        return {'h': jax.random.normal(ks[0], (N, H), jnp.float32), 'node_adj': _sign_adj(ks[1], N, 0.005), 'edge_adj': _sign_adj(ks[2], N, 0.005), 'gat_W': jax.random.normal(ks[3], (HEADS, H, H), jnp.float32) * (gain / np.sqrt(H, dtype=np.float32)), 'gat_a': jax.random.normal(ks[4], (HEADS, 2 * H, 1), jnp.float32) * 0.1, 'edge_Wih': jax.random.normal(ks[5], (3 * H, H), jnp.float32) * std, 'edge_Whh': jax.random.normal(ks[6], (3 * H, H), jnp.float32) * std, 'edge_bih': jnp.zeros((3 * H,), jnp.float32), 'edge_bhh': jnp.zeros((3 * H,), jnp.float32), 'node_Wih': jax.random.normal(ks[7], (3 * H, H), jnp.float32) * std, 'node_Whh': jax.random.normal(ks[8], (3 * H, H), jnp.float32) * std, 'node_bih': jnp.zeros((3 * H,), jnp.float32), 'node_bhh': jnp.zeros((3 * H,), jnp.float32)}
    _L0_gnn_all = _L0_gnn_setup()
    _L0_gnn_in = {k: v for k, v in _L0_gnn_all.items() if k in ('gat_W', 'gat_a', 'edge_Wih', 'edge_Whh', 'edge_bih', 'edge_bhh', 'node_Wih', 'node_Whh', 'node_bih', 'node_bhh', )}
    del _L0_gnn_all

    def _L1_gnn_setup():
        import jax, jax.numpy as jnp
        import numpy as np
        N = 4096
        IN_F = 256
        OUT_F = 64
        H = 4
        NEG_SLOPE = 0.2
        key = jax.random.key(seed)
        k1, k2, k3, k4 = jax.random.split(key, 4)
        x = jax.random.normal(k1, (N, IN_F), dtype=jnp.float32)
        adj = jax.random.randint(k2, (N, N), 0, 2).astype(jnp.float32)
        limW = float(np.sqrt(6.0 / (IN_F + OUT_F)))
        W = jax.random.uniform(k3, (H, IN_F, OUT_F), minval=-limW, maxval=limW, dtype=jnp.float32)
        lima = float(np.sqrt(6.0 / (2 * OUT_F + 1)))
        a = jax.random.uniform(k4, (H, 2 * OUT_F, 1), minval=-lima, maxval=lima, dtype=jnp.float32)
        return {'x': x, 'adj': adj, 'W': W, 'a': a}
    _L1_gnn_all = _L1_gnn_setup()
    _L1_gnn_in = {k: v for k, v in _L1_gnn_all.items() if k in ('W', 'a', )}
    del _L1_gnn_all

    return {
        "x": x,
        "adj": adj,
        "L0_gnn_gat_W": _L0_gnn_in["gat_W"],
        "L0_gnn_gat_a": _L0_gnn_in["gat_a"],
        "L0_gnn_edge_Wih": _L0_gnn_in["edge_Wih"],
        "L0_gnn_edge_Whh": _L0_gnn_in["edge_Whh"],
        "L0_gnn_edge_bih": _L0_gnn_in["edge_bih"],
        "L0_gnn_edge_bhh": _L0_gnn_in["edge_bhh"],
        "L0_gnn_node_Wih": _L0_gnn_in["node_Wih"],
        "L0_gnn_node_Whh": _L0_gnn_in["node_Whh"],
        "L0_gnn_node_bih": _L0_gnn_in["node_bih"],
        "L0_gnn_node_bhh": _L0_gnn_in["node_bhh"],
        "L1_gnn_W": _L1_gnn_in["W"],
        "L1_gnn_a": _L1_gnn_in["a"],
    }

def reference(x, adj, L0_gnn_gat_W, L0_gnn_gat_a, L0_gnn_edge_Wih, L0_gnn_edge_Whh, L0_gnn_edge_bih, L0_gnn_edge_bhh, L0_gnn_node_Wih, L0_gnn_node_Whh, L0_gnn_node_bih, L0_gnn_node_bhh, L1_gnn_W, L1_gnn_a):
    import jax
    import jax.numpy as jnp
    def _L0_gnn_ref(h, node_adj, edge_adj, gat_W, gat_a, edge_Wih, edge_Whh, edge_bih, edge_bhh, node_Wih, node_Whh, node_bih, node_bhh):
        import jax, jax.numpy as jnp
        import numpy as np
        N, H, HEADS = (4096, 256, 3)
        ALPHA = 0.2
        NEG_INF = -9000000000000000.0

        def _sign_adj(key, n, density):
            k1, k2 = jax.random.split(key)
            mask = jax.random.uniform(k1, (n, n)) < density
            sign = jnp.where(jax.random.uniform(k2, (n, n)) < 0.5, -1.0, 1.0)
            adj = jnp.where(mask, sign, 0.0).astype(jnp.float32)
            idx = jnp.arange(n)
            return adj.at[idx, idx].set(1.0)

        def _gru_cell(x, hstate, Wih, Whh, bih, bhh):
            gi = x @ Wih.T + bih
            gh = hstate @ Whh.T + bhh
            ir, iz, inn = jnp.split(gi, 3, axis=1)
            hr, hz, hn = jnp.split(gh, 3, axis=1)
            r = jax.nn.sigmoid(ir + hr)
            z = jax.nn.sigmoid(iz + hz)
            n = jnp.tanh(inn + r * hn)
            return (1.0 - z) * n + z * hstate

        def _gat_head(h, node_adj, edge_adj, W, a):
            hW = h @ W
            hp = (node_adj > 0).astype(hW.dtype) @ hW
            hm = (node_adj < 0).astype(hW.dtype) @ hW
            e_plus = jax.nn.leaky_relu(jnp.concatenate([hp, hm], axis=1) @ a, ALPHA)[:, 0]
            e_minus = jax.nn.leaky_relu(jnp.concatenate([hm, hp], axis=1) @ a, ALPHA)[:, 0]
            att = jnp.where(edge_adj > 0, e_plus[None, :], NEG_INF)
            att = jnp.where(edge_adj < 0, e_minus[None, :], att)
            att = jax.nn.softmax(att, axis=1)
            return att * edge_adj @ hW
        dn = jnp.diag(node_adj)
        de = jnp.diag(edge_adj)
        idx = jnp.arange(node_adj.shape[0])
        node_adj_norm = node_adj.at[idx, idx].add(-dn)
        edge_adj_norm = edge_adj.at[idx, idx].add(-de)
        node_support = node_adj_norm @ h
        edge_output = _gru_cell(node_support, h, edge_Wih, edge_Whh, edge_bih, edge_bhh)
        edge_support = _gat_head(h, node_adj_norm, edge_adj_norm, gat_W[0], gat_a[0])
        for i in range(1, HEADS):
            edge_support = edge_support + _gat_head(h, node_adj_norm, edge_adj_norm, gat_W[i], gat_a[i])
        edge_support = edge_support / HEADS
        node_output = _gru_cell(edge_support, h, node_Wih, node_Whh, node_bih, node_bhh)
        return de[:, None] * edge_output + dn[:, None] * node_output

    def _L1_gnn_ref(x, adj, W, a):
        import jax, jax.numpy as jnp
        import numpy as np
        N = 4096
        IN_F = 256
        OUT_F = 64
        H = 4
        NEG_SLOPE = 0.2
        n = x.shape[0]
        h, _, fo = W.shape
        Wh = jnp.einsum('nd,hdo->nho', x, W)
        a_src = a[:, :fo, 0]
        a_dst = a[:, fo:, 0]
        s_i = jnp.einsum('nho,ho->nh', Wh, a_src)
        s_j = jnp.einsum('nho,ho->nh', Wh, a_dst)
        e = jax.nn.leaky_relu(s_i[:, None, :] + s_j[None, :, :], NEG_SLOPE)
        idx = jnp.arange(n)
        adj_sl = adj.at[idx, idx].set(1.0)
        mask = (adj_sl != 0)[:, :, None]
        e_masked = jnp.where(mask, e, -jnp.inf)
        attention = jax.nn.softmax(e_masked, axis=1)
        h_prime = jnp.einsum('ijh,jho->iho', attention, Wh)
        return h_prime.reshape(n, h * fo)

    x = _layernorm(x + _L0_gnn_ref(x, adj, adj, L0_gnn_gat_W, L0_gnn_gat_a, L0_gnn_edge_Wih, L0_gnn_edge_Whh, L0_gnn_edge_bih, L0_gnn_edge_bhh, L0_gnn_node_Wih, L0_gnn_node_Whh, L0_gnn_node_bih, L0_gnn_node_bhh), axis=-1)
    x = _layernorm(x + _L1_gnn_ref(x, adj, L1_gnn_W, L1_gnn_a), axis=-1)
    return x


_drawn_inputs = setup_inputs


def setup_inputs(seed=0):
    import zlib

    import numpy as np

    out = dict(_drawn_inputs(seed))
    spreads = {'L0_gnn_edge_bih': (0.0, 0.362),
     'L0_gnn_edge_bhh': (0.0, 0.615),
     'L0_gnn_node_bih': (0.0, 0.301),
     'L0_gnn_node_bhh': (0.0, 0.489)}
    factors = {'L0_gnn_gat_W': 4.062,
     'L0_gnn_gat_a': 4.093,
     'L0_gnn_edge_Whh': 3.1,
     'L0_gnn_node_Wih': 4.058,
     'L0_gnn_node_Whh': 2.925}
    for name, (base, spread) in spreads.items():
        noise = np.random.default_rng([zlib.crc32(name.encode()), seed]).standard_normal(out[name].shape)
        drawn = base * np.exp(spread * noise) if base else spread * noise
        out[name] = jnp.asarray(drawn.astype(out[name].dtype))
    for name, factor in factors.items():
        out[name] = (out[name] * factor).astype(out[name].dtype)
    return out
```

```python
from contextlib import ExitStack

import numpy as np

import concourse.bass as bass
from concourse import mybir

ALU = mybir.AluOpType
ACT = mybir.ActivationFunctionType
AX = mybir.AxisListType
F32 = mybir.dt.float32
BF16 = mybir.dt.bfloat16
I32 = mybir.dt.int32

P = 128
N = 3327
JT = -(-N // P)
NP = JT * P
H = 256
KC = H // P
HEADS = 3
NV = 2 * HEADS
IB = 416
NB = NP // IB
RING = 13
HALF = JT // RING
GATES = 3 * H
CNT = 32
H1, FO = 4, 64
FP = FO + 1
IB1 = 256
NB1 = NP // IB1
IT1 = IB1 // P
PW = 3 * FP
BIG = 1e30
TINY = 1e-30
SLOPE = 0.2
EPS = 1e-5


def ds(start, size):
    return bass.ds(start, size)


class Count:

    def __init__(self, eng, sem):
        self.eng, self.sem, self.base, self.k = eng, sem, 0, 0

    def at(self, base):
        self.base, self.k = base, 0

    def link(self, ins):
        self.k += 1
        ins.then_inc(self.sem, 1)
        self.eng.wait_ge(self.sem, self.base + self.k)

    def settle(self, ins, cell):
        self.link(ins)
        self.eng.memset(cell, 0.0)


def build(nc, A, AT, x, xT, diag, W0, W0T, a0, eWi, eWh, ebi, ebh, nWi, nWh, nbi, nbh, W1, W1T, a1, sel, out):
    e_dram = nc.dram_tensor("e_dram", (NV, NP), F32, kind="Internal").ap()
    nm_dram = nc.dram_tensor("nm_dram", (HEADS, NP), F32, kind="Internal").ap()
    s_dram = nc.dram_tensor("s_dram", (H1, NP), F32, kind="Internal").ap()
    t_dram = nc.dram_tensor("t_dram", (1, 2 * H1), F32, kind="Internal").ap()

    ctx = ExitStack()
    with ctx:
        def sb(name, shape, dt=F32):
            return ctx.enter_context(nc.sbuf_tensor(name, shape, dt))

        def sem(name):
            return ctx.enter_context(nc.semaphore(name))

        yT = sb("yT", [P, KC, NP])
        offdiag = sb("offdiag", [P, 2 * NP], BF16)
        ring = sb("ring", [P, RING, IB])
        gw = sb("gw", [P, 2, KC, GATES])
        ident = sb("ident", [P, P])
        ones = sb("ones", [P, P])
        zdiag = sb("zdiag", [P, P], BF16)
        small = sb("small", [P, 640])
        flag_i = sb("flag_i", [P, 1], I32)
        WORK = 33600
        work = sb("work", [P, WORK])

        def carve(tensor, limit):
            at = [0]

            def take(shape, dt=F32):
                n = int(np.prod(shape))
                words = n if dt == F32 else n // 2
                v = tensor[:, at[0]:at[0] + words]
                at[0] += words
                assert at[0] <= limit, (at[0], limit)
                if dt == BF16:
                    v = v.bitcast(BF16)
                names = "abcde"[:len(shape)]
                if len(shape) > 1:
                    v = v.rearrange("p (%s) -> p %s" % (" ".join(names), " ".join(names)),
                                    **{c: s for c, s in zip(names, shape)})
                return v
            take.at = at
            return take

        tk = carve(small, 640)
        a0_sb = tk([KC, HEADS, 2])
        wa = tk([KC, NV])
        a1_sb = tk([H1, 2])
        bi = tk([6])
        bh = tk([6])
        brz = tk([4])
        ecol = tk([JT, NV])
        nm = tk([HEADS * JT])
        mcol = tk([JT, HEADS])
        mneg = tk([1])
        mrow = tk([2, HEADS])
        cell = tk([1])
        flag = tk([1])
        stats = tk([2, 6])
        mv = tk([2, 2])
        sd = tk([2, 1])
        rstd = tk([2, 1])
        eps = tk([1])
        tmax = tk([1])
        tb = tk([2 * H1])
        st = tk([JT, 2 * H1])

        def gru_buffers(tk):
            return [tk([IB]) for _ in range(6)]

        tk = carve(work, WORK)
        x_sb = tk([JT, H])
        escore = tk([NP])
        am = tk([2, IB])
        pos = tk([2, IB], BF16)
        neg = tk([2, IB], BF16)
        nsT = tk([KC, IB])
        usum = tk([2, IB])
        zs = tk([IB])
        gru1 = gru_buffers(tk)
        w0t = tk([HEADS * KC, H])
        w1t = tk([H1, H])
        u_sb = tk([JT, NV])
        u_r = tk([JT, NV])
        upar = tk([JT, 20], BF16)
        sel_sb = tk([2, CNT + 1])
        diag1 = tk([IB])

        tk = carve(work, WORK)
        ebc = tk([NV, NP])
        a2 = tk([2, NP])
        junk = tk([NP])
        pen2 = tk([NP], BF16)
        nmT = tk([P])

        tk = carve(work, WORK)
        hw = tk([JT, HEADS * H])
        xt2 = tk([KC, NP])
        w0 = tk([KC, HEADS * H])
        tk.at[0] = JT * HEADS * H
        wgt = tk([2, HEADS, IB])
        u = tk([2, HEADS, IB])
        wacc = tk([HEADS, IB])
        negm = tk([HEADS, IB])
        esT = tk([KC, IB])
        xTb = tk([KC, IB])
        diag3 = tk([IB])
        mask3 = tk([IB], BF16)
        pen3 = tk([IB], BF16)
        rden = tk([IB])
        argn = rden
        gru3 = gru_buffers(tk)

        tk = carve(work, WORK)
        x1 = tk([JT, H])
        early = tk.at[0]
        parts = tk([JT, H1, 2, 3, FP], BF16)
        spare = tk.at[0]
        wh = tk([JT, H])
        tk = carve(work, WORK)
        tk.at[0] = early
        strow = tk([NP])
        ys = tk([2, KC, P])
        xs = tk([2, H])
        x1T = tk([2, KC, P])
        tk = carve(work, WORK)
        tk.at[0] = spare
        sbc = tk([H1, IB1])
        g = tk([2, 2, H1, IB1], BF16)
        ev = tk([IT1, H1, 2 * PW])
        tky = carve(yT[:, :, :].rearrange("p a b -> p (a b)"), KC * NP)
        bcoef = tky([JT, H1, 2])
        acoef = tky([2, JT, H1])
        ush = tky([JT, H1])
        negt = tky([JT, H1])
        fx = tky([2, H1, 2, FP])
        mask5 = tky([2, IB1], BF16)
        xsum = tky([H1, 2, FP])
        tmp5 = tky([H1, FP])
        num = tky([H1, FP])
        rd1 = tky([H1])
        y5 = tky([2, H])
        o5 = tky([2, H])
        stat5 = tky([6])
        mv5 = tky([2])
        sd5 = tky([1])
        rs5 = tky([1])
        tkw = carve(gw[:, :, :, :].rearrange("p a b c -> p (a b c)"), 2 * KC * GATES)
        wall = tkw([KC, H + 2 * H1])
        wa1 = sb("wa1", [P, KC, 2 * H1])

        bank = [ctx.enter_context(nc.psum_tensor(f"bank{i}", [P, 512], F32)) for i in range(8)]

        const_ready, vec_chain, pool_chain = sem("const_ready"), sem("vec_chain"), sem("pool_chain")
        support_chain, norm_chain, parts_chain, gat_chain = [sem(n + "_chain") for n in ("support", "norm", "parts", "gat")]
        rowmax_chain = [sem("rowmax_chain"), sem("rowmax_chain_signed")]
        attend_chain = [sem("attend_chain"), sem("attend_chain_signed")]
        setup_loaded, x_loaded, xT_loaded, egw_loaded = sem("setup_loaded"), sem("x_loaded"), sem("xT_loaded"), sem("egw_loaded")
        wa_done, wa_ready, u_done, upar_ready = sem("wa_done"), sem("wa_ready"), sem("u_done"), sem("upar_ready")
        tile_loaded = [sem(f"tile_loaded{i}") for i in range(RING)]
        support_in, support_mm, support_evac = sem("support_in"), sem("support_mm"), sem("support_evac")
        sel_done, zs_ready, e_ready = sem("sel_done"), sem("zs_ready"), sem("e_ready")
        diag_loaded, bias_ready = sem("diag_loaded"), sem("bias_ready")
        G = [{k: sem(f"{k}_{p}") for k in ("gate_mm", "r_read", "z_read", "hn_read", "pre_ready", "n_ready", "out_ready", "gru_done")}
             for p in ("edge", "node")]
        e_stored, ebc_loaded, a2_loaded = sem("e_stored"), sem("ebc_loaded"), [sem("a2_loaded0"), sem("a2_loaded1")]
        ecol_mm, ecol_ready, flag_ready, rowmax_done = sem("ecol_mm"), sem("ecol_ready"), sem("flag_ready"), sem("rowmax_done")
        nm_ready, nm_mm, nmT_ready, nm_stored = sem("nm_ready"), sem("nm_mm"), sem("nmT_ready"), sem("nm_stored")
        xt2_loaded, hw_mm, hw_evac_a, hw_evac_v = sem("xt2_loaded"), sem("hw_mm"), sem("hw_evac_a"), sem("hw_evac_v")
        ngw_loaded, negm_loaded, xTb_loaded = sem("ngw_loaded"), sem("negm_loaded"), sem("xTb_loaded")
        arg_ready, wgt_ready, u_ready, attend_mm, wacc_ready = [sem(n) for n in ("arg_ready", "wgt_ready", "u_ready", "attend_mm", "wacc_ready")]
        den_mm, den_read, es_ready = sem("den_mm"), sem("den_read"), sem("es_ready")
        wall_loaded = sem("wall_loaded")
        ys_ready, yt_mm, var_ready, sd_ready, xs_ready, x1_stored, x1T_mm, x1T_ready, wh_mm, wh_ready, strow_ready = [
            sem(n) for n in ("ys_ready", "yt_mm", "var_ready", "sd_ready", "xs_ready", "x1_stored", "x1T_mm",
                             "x1T_ready", "wh_mm", "wh_ready", "strow_ready")]
        tmax_ready, s_stored, tb_loaded, ush_ready, coef_ready, fx_ready, parts_ready = [
            sem(n) for n in ("tmax_ready", "s_stored", "tb_loaded", "ush_ready", "coef_ready", "fx_ready", "parts_ready")]
        sbc_loaded, g_ready, gat_mm, ev_ready, xsum_ready, num_ready, var5, sd5_ready, o_ready, o_stored = [
            sem(n) for n in ("sbc_loaded", "g_ready", "gat_mm", "ev_ready", "xsum_ready", "num_ready", "var5",
                             "sd5_ready", "o_ready", "o_stored")]

        def window(j, i0, width):
            return offdiag[:, ds(i0 + (NP - P * j), width)]

        block = ctx.enter_context(nc.Block())

        @block.sync
        def _(sp):
            for dst, src in ((w0t, W0T.rearrange("(t p) k -> p t k", p=P)),
                             (a0_sb, a0.rearrange("(c p) h s -> p c h s", p=P)),
                             (w1t[0:FO], W1T), (a1_sb[0:FO], a1), (bi, ebi), (bh, ebh), (sel_sb[0:19], sel)):
                sp.dma_start(dst, src).then_inc(setup_loaded, 16)
            sp.dma_start(yT[:, :, :], xT.rearrange("(c p) n -> p c n", p=P)).then_inc(xT_loaded, 16)
            sp.dma_start(x_sb, x.rearrange("(t p) f -> p t f", p=P)).then_inc(x_loaded, 16)

            def load_tile(i0, j, width=IB):
                sp.dma_start(ring[:, j % RING, 0:width],
                             AT[P * j:P * (j + 1), ds(i0, width)]).then_inc(tile_loaded[j % RING], 16)

            def stream(used, blocks, width, extra):
                for j in range(RING):
                    load_tile(0, j, width)
                extra(0)
                with sp.Fori(0, blocks - 1) as b:
                    for j in range(RING, JT):
                        sp.wait_ge(used, b * JT + (j - RING + 1))
                        load_tile(b * width, j, width)
                    for j in range(RING):
                        sp.wait_ge(used, b * JT + (RING + j + 1))
                        load_tile((b + 1) * width, j, width)
                    extra(b + 1)
                for j in range(RING, JT):
                    sp.wait_ge(used, (blocks - 1) * JT + (j - RING + 1))
                    load_tile((blocks - 1) * width, j, width)

            sp.dma_start(gw[:, 0, :, :], eWi.rearrange("(c p) n -> p c n", p=P)).then_inc(egw_loaded, 16)
            sp.dma_start(gw[:, 1, :, :], eWh.rearrange("(c p) n -> p c n", p=P)).then_inc(egw_loaded, 16)

            def support_extra(b):
                if not (isinstance(b, int) and b == 0):
                    sp.wait_ge(G[0]["gru_done"], b * KC)
                sp.dma_start(diag1, diag[:, ds(b * IB, IB)].partition_broadcast(P).rearrange("p a n -> p (a n)")
                             ).then_inc(diag_loaded, 16)

            stream(support_in, NB, IB, support_extra)

            sp.wait_ge(e_ready, NB)
            sp.dma_start(e_dram, escore[0:NV, :]).then_inc(e_stored, 16)
            sp.wait_ge(e_stored, 16)
            sp.wait_ge(ecol_mm, 1)
            sp.wait_ge(flag_ready, 1)
            sp.wait_ge(support_mm, NB * JT)
            sp.wait_ge(G[0]["gru_done"], NB * KC)
            sp.dma_start(ebc, e_dram.partition_broadcast(P)).then_inc(ebc_loaded, 16)
            for k in range(2):
                sp.dma_start(a2[:, k, :], A[k * P:(k + 1) * P, :]).then_inc(a2_loaded[k], 16)
            with sp.Fori(0, JT // 2 - 1) as t:
                for k in range(2):
                    sp.wait_ge(rowmax_done, 2 * t + (k + 1))
                    sp.dma_start(a2[:, k, :], A[ds((2 * t + (2 + k)) * P, P), :]).then_inc(a2_loaded[k], 16)

            sp.wait_ge(rowmax_done, JT)
            sp.dma_start(xt2, xT.rearrange("(c p) n -> p c n", p=P)).then_inc(xt2_loaded, 16)
            sp.dma_start(w0, W0.rearrange("(c p) n -> p c n", p=P)).then_inc(xt2_loaded, 16)
            for dst, src in ((gw[:, 0, :, :], nWi.rearrange("(c p) n -> p c n", p=P)),
                             (gw[:, 1, :, :], nWh.rearrange("(c p) n -> p c n", p=P)), (bi, nbi), (bh, nbh)):
                sp.dma_start(dst, src).then_inc(ngw_loaded, 16)
            sp.wait_ge(nmT_ready, 1)
            sp.dma_start(nm_dram.rearrange("h (t p) -> (h t) p", p=P), nmT[0:HEADS * JT, :]).then_inc(nm_stored, 16)
            sp.wait_ge(nm_stored, 16)
            sp.wait_ge(hw_mm, 2 * JT)

            def attend_extra(b):
                first = isinstance(b, int) and b == 0
                if not first:
                    sp.wait_ge(arg_ready, b * JT * HEADS)
                sp.dma_start(negm, nm_dram[:, ds(b * IB, IB)].partition_broadcast(P)).then_inc(negm_loaded, 16)
                if not first:
                    sp.wait_ge(G[1]["gru_done"], b * KC)
                sp.dma_start(diag3, diag[:, ds(b * IB, IB)].partition_broadcast(P).rearrange("p a n -> p (a n)")
                             ).then_inc(xTb_loaded, 16)
                sp.dma_start(xTb, xT.rearrange("(c p) n -> p c n", p=P)[:, :, ds(b * IB, IB)]).then_inc(xTb_loaded, 16)

            stream(u_ready, NB, IB, attend_extra)

            sp.wait_ge(G[1]["gate_mm"], NB * KC * 4)
            sp.dma_start(wall[:, :, 0:H], W1.rearrange("(c p) n -> p c n", p=P)).then_inc(wall_loaded, 16)
            sp.wait_ge(strow_ready, JT)
            sp.dma_start(s_dram, strow[0:H1, :]).then_inc(s_stored, 16)
            sp.wait_ge(tmax_ready, 1)
            sp.dma_start(t_dram.rearrange("a h -> h a"), tmax[0:2 * H1, :]).then_inc(s_stored, 16)
            sp.wait_ge(s_stored, 32)
            sp.dma_start(tb, t_dram.partition_broadcast(P).rearrange("p a n -> p (a n)")).then_inc(tb_loaded, 16)

            def gat_extra(b):
                if not (isinstance(b, int) and b == 0):
                    sp.wait_ge(g_ready, b * JT)
                sp.dma_start(sbc, s_dram[:, ds(b * IB1, IB1)].partition_broadcast(P)).then_inc(sbc_loaded, 16)

            sp.wait_ge(parts_ready, JT)
            stream(g_ready, NB1, IB1, gat_extra)
            sp.wait_ge(o_stored, 16 * JT)

        def pe_gru(pe, S, b, inT, hT, weights):
            for c in range(KC):
                q = b * KC + c

                def gate(dst, m, sources):
                    terms = [(s, kc) for s in sources for kc in range(KC)]
                    for n, (s, kc) in enumerate(terms):
                        mm = pe.matmul(dst[:, 0:IB], weights[:, s, kc, m * P:(m + 1) * P], (inT, hT)[s](kc),
                                       start=(n == 0), stop=(n == len(terms) - 1))
                    mm.then_inc(S["gate_mm"], 1)

                if c > 0:
                    pe.wait_ge(S["hn_read"], q)
                gate(bank[6], c, (0, 1))
                if c > 0:
                    pe.wait_ge(S["pre_ready"], q)
                gate(bank[7], KC + c, (0, 1))
                pe.wait_ge(S["r_read"], q + 1)
                gate(bank[6], 2 * KC + c, (1,))
                pe.wait_ge(S["z_read"], q + 1)
                gate(bank[7], 2 * KC + c, (0,))
            pe.wait_ge(S["hn_read"], b * KC + KC)
            pe.wait_ge(S["pre_ready"], b * KC + KC)

        def act_gru(act, S, b, buf):
            tr, tz, hq, nn, _, _ = buf
            for c in range(KC):
                q = b * KC + c
                if c > 0:
                    act.wait_ge(S["out_ready"], q)
                act.wait_ge(S["gate_mm"], 4 * q + 1)
                act.activation(tr, bank[6][:, 0:IB], ACT.Tanh, bias=brz[:, c:c + 1], scale=0.5).then_inc(S["r_read"], 1)
                act.wait_ge(S["gate_mm"], 4 * q + 2)
                act.activation(tz, bank[7][:, 0:IB], ACT.Tanh, bias=brz[:, KC + c:KC + c + 1],
                               scale=0.5).then_inc(S["z_read"], 1)
                act.wait_ge(S["gate_mm"], 4 * q + 3)
                act.activation(hq, bank[6][:, 0:IB], ACT.Identity, bias=bh[:, 4 + c:5 + c]).then_inc(S["hn_read"], 1)
                act.wait_ge(S["pre_ready"], q + 1)
                act.activation(nn, hq, ACT.Tanh, bias=bi[:, 4 + c:5 + c]).then_inc(S["n_ready"], 1)
            act.wait_ge(S["out_ready"], b * KC + KC)

        GRU_LINKS = 4 * KC

        def vec_gru(dve, S, b, buf, xin, dg, chain):
            tr, tz, hq, nn = buf[:4]
            for c in range(KC):
                q, dx = b * KC + c, buf[4 + c]
                dve.wait_ge(S["hn_read"], q + 1)
                chain.link(dve.scalar_tensor_tensor(hq, tr, 1.0, hq, ALU.add, ALU.mult))
                dve.wait_ge(S["gate_mm"], 4 * q + 4)
                dve.scalar_tensor_tensor(hq, hq, 0.5, bank[7][:, 0:IB], ALU.mult, ALU.add).then_inc(S["pre_ready"], 1)
                dve.wait_ge(S["n_ready"], q + 1)
                chain.link(dve.tensor_tensor(dx, xin(c), nn, ALU.subtract))
                chain.link(dve.scalar_tensor_tensor(dx, tz, 1.0, dx, ALU.add, ALU.mult))
                ins = dve.scalar_tensor_tensor(dx, dx, 0.5, nn, ALU.mult, ALU.add)
                ins.then_inc(S["out_ready"], 1)
                dve.wait_ge(S["out_ready"], q + 1)
                chain.link(dve.tensor_tensor(dx, dx, dg, ALU.mult))
            dve.wait_ge(S["gate_mm"], b * (4 * KC) + 4 * KC)
            for c in range(KC):
                y = yT[:, c, ds(b * IB, IB)]
                dve.tensor_tensor(y, y, buf[4 + c], ALU.add).then_inc(S["gru_done"], 1)

        @block.tensor
        def _(pe):
            pe.wait_ge(setup_loaded, 16 * 7)
            for h in range(HEADS):
                for kc in range(KC):
                    for oc in range(KC):
                        pe.matmul(bank[0][:, kc * NV + 2 * h:kc * NV + 2 * h + 2],
                                  w0t[:, h * KC + oc, kc * P:(kc + 1) * P], a0_sb[:, oc, h, :],
                                  start=(oc == 0), stop=(oc == KC - 1))
            for h in range(H1):
                for kc in range(KC):
                    o = kc * 2 * H1 + 2 * h
                    mm = pe.matmul(bank[1][:, o:o + 2], w1t[0:FO, h, kc * P:(kc + 1) * P], a1_sb[0:FO, h, :],
                                   start=True, stop=True)
            mm.then_inc(wa_done, 1)
            pe.wait_ge(wa_ready, 1)
            pe.wait_ge(xT_loaded, 16)
            for t in range(JT):
                for kc in range(KC):
                    mm = pe.matmul(bank[2][:, t * NV:(t + 1) * NV], yT[:, kc, t * P:(t + 1) * P], wa[:, kc, :],
                                   start=(kc == 0), stop=(kc == KC - 1))
            mm.then_inc(u_done, 1)

            pe.wait_ge(upar_ready, 1)
            pe.wait_ge(x_loaded, 16)
            pe.wait_ge(egw_loaded, 32)
            with pe.Fori(0, NB) as b:
                for j in range(JT):
                    pe.wait_ge(support_in, b * JT + (j + 1))
                    first, last = j == 0, j == JT - 1
                    for c in range(KC):
                        pe.matmul(bank[c][:, 0:IB], x_sb[:, j, c * P:(c + 1) * P], am[:, j % 2, :], start=first, stop=last)
                    pe.matmul(bank[2][0:19, 0:IB], upar[:, j, 0:19], pos[:, j % 2, :], start=first, stop=last)
                    pe.matmul(bank[3][0:19, 0:IB], upar[:, j, 0:19], neg[:, j % 2, :], start=first,
                              stop=last).then_inc(support_mm, 1)
                pe.wait_ge(support_evac, 4 * b + 4)
                pe.matmul(bank[4][0:CNT + 1, 0:IB], sel_sb[0:19, 0, :], usum[0:19, 0, :], start=True, stop=False)
                pe.matmul(bank[4][0:CNT + 1, 0:IB], sel_sb[0:19, 1, :], usum[0:19, 1, :], start=False,
                          stop=True).then_inc(sel_done, 1)
                pe_gru(pe, G[0], b, lambda kc: nsT[:, kc, :], lambda kc: yT[:, kc, ds(b * IB, IB)], gw)
                pe.wait_ge(zs_ready, b + 1)

            pe.wait_ge(e_ready, NB)
            for t in range(JT):
                mm = pe.transpose(bank[5][:, t * NV:(t + 1) * NV], escore[0:NV, t * P:(t + 1) * P], ident[0:NV, 0:NV])
            mm.then_inc(ecol_mm, 1)
            pe.wait_ge(nm_ready, 1)
            pe.transpose(bank[4][0:HEADS * JT, 0:P], nm, ident[:, :]).then_inc(nm_mm, 1)

            pe.wait_ge(xt2_loaded, 32)
            pe.wait_ge(ecol_ready, 1)
            pe.wait_ge(nmT_ready, 1)
            half = HEADS * H // 2
            for t in range(JT):
                for n in range(2):
                    if t >= 4:
                        pe.wait_ge((hw_evac_a, hw_evac_v)[n], t - 3)
                    for kc in range(KC):
                        mm = pe.matmul(bank[(2 * t + n) % 8][:, 0:half], xt2[:, kc, t * P:(t + 1) * P],
                                       w0[:, kc, n * half:(n + 1) * half], start=(kc == 0), stop=(kc == KC - 1))
                    mm.then_inc(hw_mm, 1)

            pe.wait_ge(hw_evac_a, JT)
            pe.wait_ge(hw_evac_v, JT)
            pe.wait_ge(ngw_loaded, 64)
            with pe.Fori(0, NB) as b:
                for j in range(JT):
                    pe.wait_ge(u_ready, b * JT + (j + 1))
                    for h in range(HEADS):
                        for c in range(KC):
                            mm = pe.matmul(bank[KC * h + c][:, 0:IB], hw[:, j, h * H + c * P:h * H + (c + 1) * P],
                                           u[:, j % 2, h, :], start=(j == 0), stop=(j == JT - 1))
                    mm.then_inc(attend_mm, 1)
                pe.wait_ge(wacc_ready, JT * b + JT)
                for h in range(HEADS):
                    if h == 2:
                        pe.wait_ge(den_read, HEADS * b + 1)
                    pe.matmul(bank[6 + h % 2][:, 0:IB], ones[:, :], wacc[:, h, :], start=True, stop=True).then_inc(den_mm, 1)
                pe.wait_ge(es_ready, b + 1)
                pe.wait_ge(xTb_loaded, 32 * b + 32)
                pe_gru(pe, G[1], b, lambda kc: esT[:, kc, :], lambda kc: xTb[:, kc, :], gw)

            pe.wait_ge(wall_loaded, 16)
            pe.wait_ge(bias_ready, 3)
            with pe.Fori(0, JT // 2) as tt:
                for k in range(2):
                    t = 2 * tt + k
                    pe.wait_ge(ys_ready, t + 1)
                    for c in range(KC):
                        mm = pe.transpose(bank[k][:, c * P:(c + 1) * P], ys[:, k, c, :], ident[:, :])
                    mm.then_inc(yt_mm, 1)
                    pe.wait_ge(xs_ready, t + 1)
                    for c in range(KC):
                        mm = pe.transpose(bank[2 + k][:, c * P:(c + 1) * P], xs[:, k, c * P:(c + 1) * P], ident[:, :])
                    mm.then_inc(x1T_mm, 1)
                    pe.wait_ge(x1T_ready, t + 1)
                    for c in range(KC):
                        pe.matmul(bank[4 + k][:, 0:H + 2 * H1], x1T[:, k, c, :], wall[:, c, :], start=(c == 0), stop=(c == KC - 1))
                    for c in range(KC):
                        mm = pe.matmul(bank[6 + k][0:2 * H1, 0:P], wa1[:, c, :], x1T[:, k, c, :], start=(c == 0), stop=(c == KC - 1))
                    mm.then_inc(wh_mm, 1)
                pe.wait_ge(strow_ready, 2 * tt + 2)
                pe.wait_ge(wh_ready, 2 * tt + 2)

            pe.wait_ge(parts_ready, JT)
            with pe.Fori(0, NB1) as b:
                for j in range(JT):
                    pe.wait_ge(g_ready, b * JT + (j + 1))
                    for c in range(IT1):
                        for h in range(H1):
                            for q in range(2):
                                mm = pe.matmul(bank[c * H1 + h][:, q * PW:(q + 1) * PW],
                                               g[:, j % 2, q, h, c * P:(c + 1) * P],
                                               parts[:, j, h, q, :, :].rearrange("p a b -> p (a b)"),
                                               start=(j == 0 and q == 0), stop=(j == JT - 1), skip_group_check=True)
                    mm.then_inc(gat_mm, 1)
                pe.wait_ge(ev_ready, (b + 1) * (IT1 * H1))

        @block.gpsimd
        def _(pool):
            def one(shape):
                v = ones[:, 0:1]
                return (v if len(shape) == 1 else v.unsqueeze(1)).to_broadcast([P] + shape)

            pool.memset(offdiag[:, :], 1.0).then_inc(pool_chain, 1)
            pool.memset(ident[:, :], 0.0).then_inc(pool_chain, 1)
            pool.memset(zdiag[:, :], 0.0).then_inc(pool_chain, 1)
            pool.memset(ones[:, :], 1.0).then_inc(const_ready, 1)
            pool.memset(eps, EPS).then_inc(const_ready, 1)
            pool.wait_ge(pool_chain, 3)
            for v, fill in ((ident, 1.0), (zdiag, -BIG)):
                pool.affine_select(out=v[:, :], in_=v[:, :], compare_op=ALU.not_equal, fill=fill, base=0,
                                   pattern=[[-1, P]], channel_multiplier=1).then_inc(const_ready, 1)
            mid = offdiag[:, NP:NP + P]
            pool.affine_select(out=mid, in_=mid, compare_op=ALU.not_equal, fill=0.0, base=0,
                               pattern=[[-1, P]], channel_multiplier=1).then_inc(const_ready, 1)

            with pool.Fori(0, NB) as b:
                for j in range(JT):
                    pool.wait_ge(wgt_ready, (b * JT + (j + 1)) * HEADS)
                    if j == 0:
                        ins = pool.tensor_tensor(wacc, wgt[:, j % 2], one([HEADS, IB]), ALU.mult)
                    else:
                        pool.wait_ge(wacc_ready, b * JT + j)
                        ins = pool.tensor_tensor(wacc, wacc, wgt[:, j % 2], ALU.add)
                    ins.then_inc(wacc_ready, 1)
                pool.wait_ge(den_mm, b * HEADS + HEADS)

            with pool.Fori(0, JT // 2) as tt:
                for k in range(2):
                    t = 2 * tt + k
                    pool.wait_ge(xs_ready, t + 1)
                    pool.tensor_tensor(x1[:, t, :], xs[:, k, :], one([H]), ALU.mult).then_inc(x1_stored, 1)

            pool.wait_ge(coef_ready, 4)
            pool.wait_ge(wh_ready, JT)
            pool.wait_ge(ys_ready, JT)
            with pool.Fori(0, JT // 2) as tt:
                for k in range(2):
                    t = 2 * tt + k
                    for q in range(2):
                        pool.tensor_tensor(fx[:, k, :, q, 0:FO], wh[:, t, :].rearrange("p (h o) -> p h o", h=H1),
                                           bcoef[:, t, :, q:q + 1].to_broadcast([P, H1, FO]), ALU.mult)
                    pool.tensor_tensor(fx[:, k, :, :, FO:FP].rearrange("p h q o -> p h (q o)"),
                                       bcoef[:, ds(t, 1), :, :].rearrange("p a h q -> p (a h) q"), one([H1, 2]), ALU.mult).then_inc(fx_ready, 1)
                pool.wait_ge(parts_ready, 2 * tt + 2)

            with pool.Fori(0, NB1) as b:
                for c in range(IT1):
                    t = IT1 * b + c
                    pool.wait_ge(ev_ready, H1 * (t + 1))
                    if c > 0:
                        pool.wait_ge(num_ready, t)
                    e = ev[:, c].rearrange("p h (q s o) -> p (h q) s o", q=2, s=3)
                    xq = xsum.rearrange("p h q o -> p (h q) o")
                    pool.tensor_tensor(xq, e[:, :, 1, :], e[:, :, 2, :], ALU.add).then_inc(xsum_ready, 1)
                    pool.wait_ge(xsum_ready, 2 * t + 1)
                    pool.tensor_tensor(xq, xq, e[:, :, 0, :], ALU.add).then_inc(xsum_ready, 1)
                pool.wait_ge(num_ready, b * IT1 + IT1)

        @block.scalar
        def _(act):
            act.wait_ge(bias_ready, 1)
            with act.Fori(0, NB) as b:
                act.wait_ge(support_mm, b * JT + JT)
                for n in range(2):
                    act.copy(usum[0:19, n, :], bank[2 + n][0:19, 0:IB]).then_inc(support_evac, 1)
                for c in range(KC):
                    act.copy(nsT[:, c, :], bank[c][:, 0:IB]).then_inc(support_evac, 1)
                act.wait_ge(sel_done, b + 1)
                act.copy(zs[0:CNT + 1, :], bank[4][0:CNT + 1, 0:IB]).then_inc(zs_ready, 1)
                act_gru(act, G[0], b, gru1)
                act.wait_ge(e_ready, b + 1)

            half = HEADS * H // 2
            act.wait_ge(rowmax_done, JT)
            for t in range(JT):
                act.wait_ge(hw_mm, 2 * t + 1)
                act.copy(hw[:, t, 0:half], bank[(2 * t) % 8][:, 0:half]).then_inc(hw_evac_a, 1)

            act.wait_ge(bias_ready, 2)
            with act.Fori(0, NB) as b:
                for j in range(JT):
                    for h in range(HEADS):
                        act.wait_ge(arg_ready, (b * JT + j) * HEADS + (h + 1))
                        act.activation(wgt[:, j % 2, h, :], wgt[:, j % 2, h, :], ACT.Exp).then_inc(wgt_ready, 1)
                act_gru(act, G[1], b, gru3)

            act.wait_ge(G[1]["gru_done"], NB * KC)
            act.wait_ge(const_ready, 5)
            with act.Fori(0, JT // 2) as tt:
                for k in range(2):
                    t = 2 * tt + k
                    act.copy(ys[:, k, :, :], yT[:, :, ds(t * P, P)]).then_inc(ys_ready, 1)
                    act.wait_ge(var_ready, t + 1)
                    act.activation(sd[:, k, :], mv[:, k, 1:2], ACT.Sqrt, bias=eps).then_inc(sd_ready, 1)
                    act.wait_ge(x1T_mm, t + 1)
                    act.copy(x1T[:, k, :, :].rearrange("p c n -> p (c n)"), bank[2 + k][:, 0:H]).then_inc(x1T_ready, 1)
                    act.wait_ge(wh_mm, t + 1)
                    act.copy(wh[:, t, :], bank[4 + k][:, 0:H])
                    act.copy(st[:, t, :], bank[4 + k][:, H:H + 2 * H1]).then_inc(wh_ready, 1)

            act.wait_ge(ush_ready, 3)
            act.activation(bcoef[:, :, :, 0], ush, ACT.Exp).then_inc(coef_ready, 1)
            act.activation(bcoef[:, :, :, 1], ush, ACT.Exp, scale=SLOPE).then_inc(coef_ready, 1)
            act.activation(acoef[:, 0, :, :], acoef[:, 0, :, :], ACT.Exp, scale=1 - SLOPE).then_inc(coef_ready, 1)
            act.activation(acoef[:, 1, :, :], acoef[:, 1, :, :], ACT.Exp, scale=SLOPE - 1).then_inc(coef_ready, 1)

            with act.Fori(0, NB1) as b:
                act.wait_ge(gat_mm, b * JT + JT)
                for c in range(IT1):
                    for h in range(H1):
                        act.copy(ev[:, c, h, :], bank[c * H1 + h][:, 0:2 * PW]).then_inc(ev_ready, 1)
                for c in range(IT1):
                    act.wait_ge(var5, IT1 * b + c + 1)
                    act.activation(sd5, mv5[:, 1:2], ACT.Sqrt, bias=eps).then_inc(sd5_ready, 1)
                    act.wait_ge(o_ready, IT1 * b + c + 1)
                    act.dma_start(out[ds((IT1 * b + c) * P, P), :], o5[:, c, :]).then_inc(o_stored, 16)

        @block.vector
        def _(dve):
            chain = Count(dve, vec_chain)
            dve.wait_ge(wa_done, 1)
            chain.link(dve.tensor_copy(wa1[:, :, :].rearrange("p c (s h) -> p c s h", s=2),
                                       bank[1][:, 0:4 * H1].rearrange("p (c h s) -> p c s h", c=KC, s=2)))
            dve.tensor_copy(wa, bank[0][:, 0:KC * NV].rearrange("p (c v) -> p c v", c=KC)).then_inc(wa_ready, 1)
            dve.wait_ge(setup_loaded, 16 * 7)
            chain.link(dve.tensor_tensor(brz, bi[:, 0:4], bh[:, 0:4], ALU.add))
            dve.tensor_scalar(brz, brz, 0.5, None, ALU.mult).then_inc(bias_ready, 1)
            dve.wait_ge(u_done, 1)
            chain.link(dve.tensor_copy(u_sb, bank[2][:, 0:JT * NV].rearrange("p (t v) -> p t v", v=NV)))
            chain.link(dve.memset(upar[:, :, 18:20], 1.0))
            chain.link(dve.tensor_copy(upar[:, :, 0:NV], u_sb))
            chain.link(dve.tensor_tensor(u_r, u_sb, upar[:, :, 0:NV], ALU.subtract))
            chain.link(dve.tensor_copy(upar[:, :, NV:2 * NV], u_r))
            chain.link(dve.tensor_tensor(u_r, u_r, upar[:, :, NV:2 * NV], ALU.subtract))
            dve.tensor_copy(upar[:, :, 2 * NV:3 * NV], u_r).then_inc(upar_ready, 1)

            dve.wait_ge(const_ready, 5)
            dve.wait_ge(xT_loaded, 16)
            loop = Count(dve, support_chain)
            with dve.Fori(0, NB) as b:
                loop.at(b * (JT + GRU_LINKS))
                for j in range(JT):
                    dve.wait_ge(tile_loaded[j % RING], 16 * (HALF * b + (j // RING + 1)))
                    if j >= 2:
                        dve.wait_ge(support_mm, b * JT + (j - 1))
                    loop.link(dve.tensor_tensor(am[:, j % 2, :], ring[:, j % RING, :], window(j, b * IB, IB), ALU.mult))
                    dve.tensor_scalar(pos[:, j % 2, :], am[:, j % 2, :], 0.0, None, ALU.is_gt)
                    dve.tensor_scalar(neg[:, j % 2, :], am[:, j % 2, :], 0.0, None, ALU.is_lt).then_inc(support_in, 1)
                dve.wait_ge(zs_ready, b + 1)
                dve.scalar_tensor_tensor(escore[0:CNT + 1, ds(b * IB, IB)], zs[0:CNT + 1, :], SLOPE, zs[0:CNT + 1, :],
                                         ALU.mult, ALU.max).then_inc(e_ready, 1)
                dve.wait_ge(diag_loaded, 16 * (b + 1))
                vec_gru(dve, G[0], b, gru1, lambda c: yT[:, c, ds(b * IB, IB)], diag1, loop)
                assert loop.k == JT + GRU_LINKS

            dve.wait_ge(e_ready, NB)
            chain.link(dve.tensor_reduce(flag[CNT:CNT + 1, :], escore[CNT:CNT + 1, :], AX.X, ALU.max))
            dve.tensor_copy(flag_i[CNT:CNT + 1, :], flag[CNT:CNT + 1, :]).then_inc(flag_ready, 1)
            dve.wait_ge(ecol_mm, 1)
            dve.tensor_copy(ecol, bank[5][:, 0:JT * NV].rearrange("p (t v) -> p t v", v=NV)).then_inc(ecol_ready, 1)
            dve.wait_ge(flag_ready, 1)
            negatives = dve.value_load(flag_i[CNT:CNT + 1, 0:1], min_val=0, max_val=NP)

            dve.wait_ge(ebc_loaded, 16)

            def rowmax(signed):
                loop = Count(dve, rowmax_chain[signed])
                with dve.Fori(0, JT // 2) as tt:
                    loop.at(tt * (10 * (1 + signed)))
                    for k in range(2):
                        t = 2 * tt + k
                        dve.wait_ge(a2_loaded[k], 16 * (tt + 1))
                        own = pen2[:, ds(t * P, P)]
                        for sign, (op, first) in enumerate(((ALU.is_le, 0), (ALU.is_ge, HEADS))[:1 + signed]):
                            loop.link(dve.tensor_scalar(pen2, a2[:, k, :], 0.0, -BIG, op, ALU.mult))
                            loop.settle(dve.tensor_tensor(own, own, zdiag[:, :], ALU.min), cell)
                            for h in range(HEADS):
                                ins = dve.tensor_tensor_reduce(junk, ebc[:, first + h, :], pen2, 1.0, -3.0e38,
                                                               ALU.add, ALU.max, mrow[:, sign, h:h + 1])
                                loop.settle(ins, cell)
                        m = mcol[:, ds(t, 1), :].rearrange("p a h -> p (a h)")
                        if signed:
                            dve.tensor_tensor(m, mrow[:, 0, :], mrow[:, 1, :], ALU.max).then_inc(rowmax_done, 1)
                        else:
                            dve.tensor_copy(m, mrow[:, 0, :]).then_inc(rowmax_done, 1)
                    used = loop.k
                assert used == 10 * (1 + signed), used

            with dve.If(negatives > 0):
                rowmax(True)
            with dve.Else():
                rowmax(False)
            dve.wait_ge(rowmax_done, JT)
            dve.tensor_scalar(nm.rearrange("p (h t) -> p t h", h=HEADS), mcol, -1.0, None, ALU.mult).then_inc(nm_ready, 1)
            dve.wait_ge(nm_mm, 1)
            dve.tensor_copy(nmT[0:HEADS * JT, :], bank[4][0:HEADS * JT, 0:P]).then_inc(nmT_ready, 1)

            half = HEADS * H // 2
            for t in range(JT):
                dve.wait_ge(hw_mm, 2 * t + 2)
                dve.tensor_copy(hw[:, t, half:2 * half], bank[(2 * t + 1) % 8][:, 0:half]).then_inc(hw_evac_v, 1)
            dve.wait_ge(ngw_loaded, 64)
            chain.link(dve.tensor_tensor(brz, bi[:, 0:4], bh[:, 0:4], ALU.add))
            dve.tensor_scalar(brz, brz, 0.5, None, ALU.mult).then_inc(bias_ready, 1)

            dve.wait_ge(nm_stored, 16)
            DEN_LINKS = HEADS * (1 + KC) + (HEADS - 1) * KC - 1

            def attend(signed):
                loop = Count(dve, attend_chain[signed])
                STEP = 4 + 2 * HEADS if signed else 2

                def arguments(b, j):
                    s = j % 2
                    tile = ring[:, j % RING, :]
                    dve.wait_ge(tile_loaded[j % RING], 16 * (HALF * NB + HALF * b + (j // RING + 1)))
                    if j >= 2:
                        dve.wait_ge(wacc_ready, b * JT + (j - 1))
                    loop.link(dve.scalar_tensor_tensor(mask3, tile, 0.0, window(j, b * IB, IB), ALU.is_gt, ALU.mult))
                    loop.link(dve.tensor_scalar(pen3, mask3, -1.0, BIG, ALU.add, ALU.mult))
                    for h in range(HEADS):
                        ins = dve.scalar_tensor_tensor(wgt[:, s, h, :], negm[:, h, :], ecol[:, j, h:h + 1], pen3,
                                                       ALU.add, ALU.min)
                        if signed:
                            loop.link(ins)
                        else:
                            ins.then_inc(arg_ready, 1)
                    if not signed:
                        return
                    loop.link(dve.scalar_tensor_tensor(mask3, tile, 0.0, window(j, b * IB, IB), ALU.is_lt, ALU.mult))
                    loop.link(dve.tensor_scalar(pen3, mask3, -1.0, BIG, ALU.add, ALU.mult))
                    for h in range(HEADS):
                        loop.link(dve.scalar_tensor_tensor(argn, negm[:, h, :], ecol[:, j, HEADS + h:HEADS + h + 1],
                                                           pen3, ALU.add, ALU.min))
                        dve.tensor_tensor(wgt[:, s, h, :], wgt[:, s, h, :], argn, ALU.max).then_inc(arg_ready, 1)

                def products(b, j):
                    s = j % 2
                    dve.wait_ge(wgt_ready, (b * JT + (j + 1)) * HEADS)
                    if j >= 2:
                        dve.wait_ge(attend_mm, b * JT + (j - 1))
                    dve.tensor_tensor(u[:, s, :, :], wgt[:, s, :, :],
                                      ring[:, j % RING, :].unsqueeze(1).to_broadcast([P, HEADS, IB]),
                                      ALU.mult).then_inc(u_ready, 1)

                with dve.Fori(0, NB) as b:
                    dve.wait_ge(negm_loaded, 16 * (b + 1))
                    loop.at(b * (STEP * JT + DEN_LINKS + GRU_LINKS))
                    for j in range(JT + 1):
                        if j < JT:
                            arguments(b, j)
                        if j > 0:
                            products(b, j - 1)
                    dve.wait_ge(attend_mm, b * JT + JT)
                    for h in range(HEADS):
                        dve.wait_ge(den_mm, b * HEADS + (h + 1))
                        dve.tensor_scalar(rden, bank[6 + h % 2][:, 0:IB], TINY, float(HEADS), ALU.max,
                                          ALU.mult).then_inc(den_read, 1)
                        dve.wait_ge(den_read, b * HEADS + (h + 1))
                        loop.link(dve.reciprocal(rden, rden))
                        for c in range(KC):
                            num3 = bank[KC * h + c][:, 0:IB]
                            if h == 0:
                                loop.link(dve.tensor_tensor(esT[:, c, :], num3, rden, ALU.mult))
                                continue
                            loop.link(dve.tensor_tensor(gru3[4], num3, rden, ALU.mult))
                            ins = dve.tensor_tensor(esT[:, c, :], esT[:, c, :], gru3[4], ALU.add)
                            if h == HEADS - 1 and c == KC - 1:
                                ins.then_inc(es_ready, 1)
                            else:
                                loop.link(ins)
                    dve.wait_ge(xTb_loaded, 32 * (b + 1))
                    vec_gru(dve, G[1], b, gru3, lambda c: xTb[:, c, :], diag3, loop)
                    used = loop.k
                assert used == STEP * JT + DEN_LINKS + GRU_LINKS, used - STEP * JT

            with dve.If(negatives > 0):
                attend(True)
            with dve.Else():
                attend(False)

            dve.wait_ge(G[1]["gate_mm"], NB * KC * 4)
            dve.tensor_copy(wall[:, :, H:H + 2 * H1], wa1[:, :, :]).then_inc(bias_ready, 1)
            chain.link(dve.tensor_scalar(offdiag[:, :], offdiag[:, :], -1.0, 1.0, ALU.mult, ALU.add))
            loop = Count(dve, norm_chain)
            with dve.Fori(0, JT // 2) as tt:
                loop.at(tt * 4)
                for k in range(2):
                    t = 2 * tt + k
                    dve.wait_ge(yt_mm, t + 1)
                    loop.settle(dve.bn_stats(stats[:, k, :], bank[k][:, 0:H]), cell)
                    dve.bn_aggr(mv[:, k, :], stats[:, k, :]).then_inc(var_ready, 1)
                    dve.wait_ge(sd_ready, t + 1)
                    loop.link(dve.reciprocal(rstd[:, k, :], sd[:, k, :]))
                    dve.tensor_scalar(xs[:, k, :], bank[k][:, 0:H], mv[:, k, 0:1], rstd[:, k, 0:1], ALU.subtract,
                                      ALU.mult).then_inc(xs_ready, 1)
                    dve.wait_ge(wh_mm, t + 1)
                    dve.tensor_copy(strow[0:2 * H1, ds(t * P, P)], bank[6 + k][0:2 * H1, 0:P]).then_inc(strow_ready, 1)
                dve.wait_ge(x1_stored, 2 * tt + 2)

            dve.wait_ge(strow_ready, JT)
            dve.tensor_reduce(tmax[0:2 * H1, :], strow[0:2 * H1, 0:N], AX.X, ALU.max).then_inc(tmax_ready, 1)
            dve.wait_ge(tb_loaded, 16)
            dve.wait_ge(wh_ready, JT)
            dve.wait_ge(ys_ready, JT)
            s_col, t_col = st[:, :, 0:H1], st[:, :, H1:2 * H1]
            t_top = tb[:, H1:2 * H1].unsqueeze(1).to_broadcast([P, JT, H1])
            chain.link(dve.tensor_tensor(ush, t_col, t_top, ALU.subtract))
            dve.tensor_scalar(ush, ush, 0.0, None, ALU.min).then_inc(ush_ready, 1)
            chain.link(dve.tensor_tensor(acoef[:, 1, :, :], s_col, t_top, ALU.add))
            chain.link(dve.tensor_scalar(acoef[:, 0, :, :], acoef[:, 1, :, :], 0.0, None, ALU.min))
            dve.tensor_scalar(acoef[:, 1, :, :], acoef[:, 1, :, :], 0.0, None, ALU.max).then_inc(ush_ready, 1)
            dve.tensor_scalar(negt, t_col, -1.0, None, ALU.mult).then_inc(ush_ready, 1)

            dve.wait_ge(s_stored, 32)
            loop = Count(dve, parts_chain)
            with dve.Fori(0, JT // 2) as tt:
                loop.at(tt * 8)
                for k in range(2):
                    t = 2 * tt + k
                    f = fx[:, k].rearrange("p h q o -> p (h q) o")
                    part = [parts[:, t, :, :, i, :].rearrange("p h q o -> p (h q) o") for i in range(3)]
                    dve.wait_ge(fx_ready, t + 1)
                    loop.link(dve.tensor_copy(part[0], f))
                    loop.link(dve.tensor_tensor(f, f, part[0], ALU.subtract))
                    loop.link(dve.tensor_copy(part[1], f))
                    loop.link(dve.tensor_tensor(f, f, part[1], ALU.subtract))
                    dve.tensor_copy(part[2], f).then_inc(parts_ready, 1)

            dve.wait_ge(parts_ready, JT)
            loop = Count(dve, gat_chain)
            OUT_LINKS = 7
            with dve.Fori(0, NB1) as b:
                loop.at(b * (2 * JT + OUT_LINKS * IT1))
                dve.wait_ge(sbc_loaded, 16 * (b + 1))
                for j in range(JT):
                    s = j % 2
                    m = mask5[:, s, :]
                    dve.wait_ge(tile_loaded[j % RING], 16 * (2 * HALF * NB + HALF * b + (j // RING + 1)))
                    if j >= 2:
                        dve.wait_ge(gat_mm, b * JT + (j - 1))
                    loop.link(dve.scalar_tensor_tensor(m, ring[:, j % RING, 0:IB1], 0.0, window(j, b * IB1, IB1),
                                                       ALU.not_equal, ALU.max))
                    for h in range(H1):
                        ins = dve.scalar_tensor_tensor(g[:, s, 0, h, :], sbc[:, h, :], negt[:, j, h:h + 1], m,
                                                       ALU.is_gt, ALU.mult)
                    loop.link(ins)
                    dve.tensor_tensor(g[:, s, 1, :, :], m.unsqueeze(1).to_broadcast([P, H1, IB1]), g[:, s, 0, :, :],
                                      ALU.subtract).then_inc(g_ready, 1)
                for c in range(IT1):
                    t = IT1 * b + c
                    dve.wait_ge(xsum_ready, 2 * (t + 1))
                    dve.wait_ge(coef_ready, 4)
                    a_pos = acoef[:, 0, ds(t, 1), :].rearrange("p a h -> p h a").to_broadcast([P, H1, FP])
                    a_neg = acoef[:, 1, ds(t, 1), :].rearrange("p a h -> p h a").to_broadcast([P, H1, FP])
                    loop.link(dve.tensor_tensor(tmp5, xsum[:, :, 0, :], a_pos, ALU.mult))
                    loop.link(dve.tensor_tensor(num, xsum[:, :, 1, :], a_neg, ALU.mult))
                    dve.tensor_tensor(num, num, tmp5, ALU.add).then_inc(num_ready, 1)
                    dve.wait_ge(num_ready, t + 1)
                    loop.link(dve.reciprocal(rd1, num[:, :, FO:FP].rearrange("p h o -> p (h o)")))
                    y = y5[:, c, :]
                    loop.link(dve.tensor_tensor(y.rearrange("p (h o) -> p h o", h=H1), num[:, :, 0:FO],
                                                rd1.unsqueeze(2).to_broadcast([P, H1, FO]), ALU.mult))
                    dve.wait_ge(x1_stored, JT)
                    loop.link(dve.tensor_tensor(y, y, x1[:, t, :], ALU.add))
                    loop.settle(dve.bn_stats(stat5, y), cell)
                    dve.bn_aggr(mv5, stat5).then_inc(var5, 1)
                    dve.wait_ge(sd5_ready, t + 1)
                    loop.link(dve.reciprocal(rs5, sd5))
                    dve.tensor_scalar(o5[:, c, :], y, mv5[:, 0:1], rs5, ALU.subtract, ALU.mult).then_inc(o_ready, 1)
                dve.wait_ge(o_stored, b * (16 * IT1) + 16 * IT1)
                used = loop.k
            assert used == 2 * JT + 7 * IT1, used


def kernel(**inputs):
    import numpy as _np
    import concourse.bacc as _bacc
    from concourse import mybir as _mybir
    from concourse.bass_utils import run_bass_kernel_spmd as _run

    v = {k: _np.asarray(a) for k, a in inputs.items()}
    adj = _np.zeros((NP, NP), _np.float32)
    adj[:N, :N] = v["adj"]
    x = _np.zeros((NP, H), _np.float32)
    x[:N] = v["x"]
    diag = _np.zeros((1, NP), _np.float32)
    diag[0, :N] = v["adj"].diagonal()
    sel = _np.zeros((19, 2, CNT + 1), _np.float32)
    for part in range(3):
        for h in range(HEADS):
            first, second = part * NV + 2 * h, part * NV + 2 * h + 1
            sel[first, 0, h] = sel[second, 1, h] = 1.0
            sel[first, 1, HEADS + h] = sel[second, 0, HEADS + h] = 1.0
    sel[18, 1, CNT] = 1.0
    gat_W, gat_a = v["L0_gnn_gat_W"], v["L0_gnn_gat_a"]
    W1, a1 = v["L1_gnn_W"], v["L1_gnn_a"]

    def bias(b):
        return b.reshape(6, P).T

    arrays = {
        "A": adj, "AT": adj.T, "x": x, "xT": x.T, "diag": diag,
        "W0": gat_W.transpose(1, 0, 2).reshape(H, HEADS * H),
        "W0T": gat_W.transpose(0, 2, 1).reshape(HEADS * H, H),
        "a0": gat_a.reshape(HEADS, 2, H).transpose(2, 0, 1),
        "eWi": v["L0_gnn_edge_Wih"].T, "eWh": v["L0_gnn_edge_Whh"].T,
        "ebi": bias(v["L0_gnn_edge_bih"]), "ebh": bias(v["L0_gnn_edge_bhh"]),
        "nWi": v["L0_gnn_node_Wih"].T, "nWh": v["L0_gnn_node_Whh"].T,
        "nbi": bias(v["L0_gnn_node_bih"]), "nbh": bias(v["L0_gnn_node_bhh"]),
        "W1": W1.transpose(1, 0, 2).reshape(H, H), "W1T": W1.transpose(2, 0, 1),
        "a1": a1.reshape(H1, 2, FO).transpose(2, 0, 1), "sel": sel,
    }
    arrays = {k: _np.ascontiguousarray(a) for k, a in arrays.items()}
    nc = _bacc.Bacc("TRN2", target_bir_lowering=False, num_devices=1)
    args = [nc.dram_tensor(f"in_{k}", a.shape, _mybir.dt.from_np(a.dtype), kind="ExternalInput").ap()
            for k, a in arrays.items()]
    out = nc.dram_tensor("out", (NP, H), _mybir.dt.float32, kind="ExternalOutput").ap()
    build(nc, *args, out)
    r = _run(nc, [{f"in_{k}": a for k, a in arrays.items()}], core_ids=[0])
    return r.results[0]["out"][:N]
```

```python
from contextlib import ExitStack

import numpy as np

import concourse.bass as bass
from concourse import mybir

ALU = mybir.AluOpType
ACT = mybir.ActivationFunctionType
AX = mybir.AxisListType
F32 = mybir.dt.float32
BF16 = mybir.dt.bfloat16
I32 = mybir.dt.int32

P = 128
N = 3327
JT = -(-N // P)
NP = JT * P
H = 256
KC = H // P
HEADS = 3
NV = 2 * HEADS
IB = 416
NB = NP // IB
RING = 13
HALF = JT // RING
GATES = 3 * H
CNT = 32
H1, FO = 4, 64
FP = FO + 1
IB1 = 256
NB1 = NP // IB1
IT1 = IB1 // P
PW = 3 * FP
BIG = 1e30
TINY = 1e-30
STEEP = 1e30
SLOPE = 0.2
EPS = 1e-5


def ds(start, size):
    return bass.ds(start, size)


class Count:

    def __init__(self, eng, sem):
        self.eng, self.sem, self.base, self.k = eng, sem, 0, 0

    def at(self, base):
        self.base, self.k = base, 0

    def link(self, ins):
        self.k += 1
        ins.then_inc(self.sem, 1)
        self.eng.wait_ge(self.sem, self.base + self.k)

    def settle(self, ins, cell):
        self.link(ins)
        self.eng.memset(cell, 0.0)


def build(nc, A, AT, x, xT, diag, W0, W0T, a0, eWi, eWh, ebi, ebh, nWi, nWh, nbi, nbh, W1, W1T, a1, sel, out):
    e_dram = nc.dram_tensor("e_dram", (NV, NP), F32, kind="Internal").ap()
    nm_dram = nc.dram_tensor("nm_dram", (HEADS, NP), F32, kind="Internal").ap()
    s_dram = nc.dram_tensor("s_dram", (H1, NP), F32, kind="Internal").ap()
    t_dram = nc.dram_tensor("t_dram", (1, 2 * H1), F32, kind="Internal").ap()

    ctx = ExitStack()
    with ctx:
        def sb(name, shape, dt=F32):
            return ctx.enter_context(nc.sbuf_tensor(name, shape, dt))

        def sem(name):
            return ctx.enter_context(nc.semaphore(name))

        yT = sb("yT", [P, KC, NP])
        offdiag = sb("offdiag", [P, 2 * NP], BF16)
        ring = sb("ring", [P, RING, IB])
        gw = sb("gw", [P, 2, KC, GATES])
        ident = sb("ident", [P, P])
        ones = sb("ones", [P, P])
        zdiag = sb("zdiag", [P, P], BF16)
        small = sb("small", [P, 640])
        flag_i = sb("flag_i", [P, 1], I32)
        WORK = 33600
        work = sb("work", [P, WORK])

        def carve(tensor, limit):
            at = [0]

            def take(shape, dt=F32):
                n = int(np.prod(shape))
                words = n if dt == F32 else n // 2
                v = tensor[:, at[0]:at[0] + words]
                at[0] += words
                assert at[0] <= limit, (at[0], limit)
                if dt == BF16:
                    v = v.bitcast(BF16)
                names = "abcde"[:len(shape)]
                if len(shape) > 1:
                    v = v.rearrange("p (%s) -> p %s" % (" ".join(names), " ".join(names)),
                                    **{c: s for c, s in zip(names, shape)})
                return v
            take.at = at
            return take

        tk = carve(small, 640)
        a0_sb = tk([KC, HEADS, 2])
        wa = tk([KC, NV])
        a1_sb = tk([H1, 2])
        bi = tk([6])
        bh = tk([6])
        brz = tk([4])
        ecol = tk([JT, NV])
        nm = tk([HEADS * JT])
        mcol = tk([JT, HEADS])
        mneg = tk([1])
        mrow = tk([2, HEADS])
        cell = tk([1])
        flag = tk([1])
        stats = tk([2, 6])
        mv = tk([2, 2])
        sd = tk([2, 1])
        rstd = tk([2, 1])
        eps = tk([1])
        tmax = tk([1])
        tb = tk([2 * H1])
        st = tk([JT, 2 * H1])

        def gru_buffers(tk):
            return [tk([IB]) for _ in range(6)]

        tk = carve(work, WORK)
        x_sb = tk([JT, H])
        escore = tk([NP])
        am = tk([2, IB])
        pos = tk([2, IB], BF16)
        neg = tk([2, IB], BF16)
        nsT = tk([KC, IB])
        usum = tk([2, IB])
        zs = tk([IB])
        gru1 = gru_buffers(tk)
        w0t = tk([HEADS * KC, H])
        w1t = tk([H1, H])
        u_sb = tk([JT, NV])
        u_r = tk([JT, NV])
        upar = tk([JT, 20], BF16)
        sel_sb = tk([2, CNT + 1])
        diag1 = tk([IB])

        tk = carve(work, WORK)
        ebc = tk([NV, NP])
        a2 = tk([2, NP])
        junk = tk([NP])
        pen2 = tk([NP], BF16)
        nmT = tk([P])

        tk = carve(work, WORK)
        hw = tk([JT, HEADS * H])
        xt2 = tk([KC, NP])
        w0 = tk([KC, HEADS * H])
        tk.at[0] = JT * HEADS * H
        wgt = tk([2, HEADS, IB])
        u = tk([2, HEADS, IB])
        wacc = tk([HEADS, IB])
        negm = tk([HEADS, IB])
        esT = tk([KC, IB])
        xTb = tk([KC, IB])
        diag3 = tk([IB])
        mask3 = tk([IB], BF16)
        pen3 = tk([IB], BF16)
        rden = tk([IB])
        argn = rden
        gru3 = gru_buffers(tk)

        tk = carve(work, WORK)
        x1 = tk([JT, H])
        early = tk.at[0]
        parts = tk([JT, H1, 2, 3, FP], BF16)
        spare = tk.at[0]
        wh = tk([JT, H])
        tk = carve(work, WORK)
        tk.at[0] = early
        strow = tk([NP])
        ys = tk([2, KC, P])
        xs = tk([2, H])
        x1T = tk([2, KC, P])
        tk = carve(work, WORK)
        tk.at[0] = spare
        g = tk([2, 2, H1, IB1], BF16)
        ev = tk([IT1, H1, 2 * PW])
        tky = carve(yT[:, :, :].rearrange("p a b -> p (a b)"), KC * NP)
        bcoef = tky([JT, H1, 2])
        acoef = tky([2, JT, H1])
        ush = tky([JT, H1])
        tsteep = tky([JT, H1])
        fx = tky([2, H1, 2, FP])
        mask5 = tky([2, IB1], BF16)
        sbc = tky([H1, IB1])
        sg = tky([2, H1, IB1], BF16)
        xsum = tky([H1, 2, FP])
        tmp5 = tky([H1, FP])
        num = tky([H1, FP])
        rd1 = tky([H1])
        y5 = tky([IT1, H])
        o5 = tky([IT1, H])
        stat5 = tky([IT1, 6])
        mv5 = tky([IT1, 2])
        sd5 = tky([IT1])
        rs5 = tky([IT1])
        tkw = carve(gw[:, :, :, :].rearrange("p a b c -> p (a b c)"), 2 * KC * GATES)
        wall = tkw([KC, H + 2 * H1])
        wa1 = sb("wa1", [P, KC, 2 * H1])

        bank = [ctx.enter_context(nc.psum_tensor(f"bank{i}", [P, 512], F32)) for i in range(8)]

        const_ready, vec_chain, pool_chain = sem("const_ready"), sem("vec_chain"), sem("pool_chain")
        support_chain, norm_chain, parts_chain, gat_chain = [sem(n + "_chain") for n in ("support", "norm", "parts", "gat")]
        rowmax_chain = [sem("rowmax_chain"), sem("rowmax_chain_signed")]
        attend_chain = [sem("attend_chain"), sem("attend_chain_signed")]
        setup_loaded, x_loaded, xT_loaded, egw_loaded = sem("setup_loaded"), sem("x_loaded"), sem("xT_loaded"), sem("egw_loaded")
        wa_done, wa_ready, u_done, upar_ready = sem("wa_done"), sem("wa_ready"), sem("u_done"), sem("upar_ready")
        tile_loaded = [sem(f"tile_loaded{i}") for i in range(RING)]
        support_in, support_mm, support_evac = sem("support_in"), sem("support_mm"), sem("support_evac")
        sel_done, zs_ready, e_ready = sem("sel_done"), sem("zs_ready"), sem("e_ready")
        diag_loaded, bias_ready = sem("diag_loaded"), sem("bias_ready")
        G = [{k: sem(f"{k}_{p}") for k in ("gate_mm", "r_read", "z_read", "hn_read", "pre_ready", "n_ready", "out_ready", "gru_done")}
             for p in ("edge", "node")]
        e_stored, ebc_loaded, a2_loaded = sem("e_stored"), sem("ebc_loaded"), [sem("a2_loaded0"), sem("a2_loaded1")]
        ecol_mm, ecol_ready, flag_ready, rowmax_done = sem("ecol_mm"), sem("ecol_ready"), sem("flag_ready"), sem("rowmax_done")
        nm_ready, nm_mm, nmT_ready, nm_stored = sem("nm_ready"), sem("nm_mm"), sem("nmT_ready"), sem("nm_stored")
        xt2_loaded, hw_mm, hw_evac_a, hw_evac_v = sem("xt2_loaded"), sem("hw_mm"), sem("hw_evac_a"), sem("hw_evac_v")
        ngw_loaded, negm_loaded, xTb_loaded = sem("ngw_loaded"), sem("negm_loaded"), sem("xTb_loaded")
        arg_ready, wgt_ready, u_ready, attend_mm, wacc_ready = [sem(n) for n in ("arg_ready", "wgt_ready", "u_ready", "attend_mm", "wacc_ready")]
        den_mm, den_read, es_ready = sem("den_mm"), sem("den_read"), sem("es_ready")
        wall_loaded = sem("wall_loaded")
        ys_ready, yt_mm, var_ready, sd_ready, xs_ready, x1_stored, x1T_mm, x1T_ready, wh_mm, wh_ready, strow_ready = [
            sem(n) for n in ("ys_ready", "yt_mm", "var_ready", "sd_ready", "xs_ready", "x1_stored", "x1T_mm",
                             "x1T_ready", "wh_mm", "wh_ready", "strow_ready")]
        tmax_ready, s_stored, tb_loaded, ush_ready, coef_ready, fx_ready, parts_ready = [
            sem(n) for n in ("tmax_ready", "s_stored", "tb_loaded", "ush_ready", "coef_ready", "fx_ready", "parts_ready")]
        sbc_loaded, sg_ready, mask_ready, pos_ready, g_ready, gat_mm, ev_ready, num_chain, num_ready, rd_ready, y_ready, \
            var5, sd5_ready, o_ready, o_stored = [
                sem(n) for n in ("sbc_loaded", "sg_ready", "mask_ready", "pos_ready", "g_ready", "gat_mm", "ev_ready",
                                 "num_chain", "num_ready", "rd_ready", "y_ready", "var5", "sd5_ready", "o_ready",
                                 "o_stored")]
        hi_cast, mid_cast, hi_ready, mid_ready = [sem(n) for n in ("hi_cast", "mid_cast", "hi_ready", "mid_ready")]

        def window(j, i0, width):
            return offdiag[:, ds(i0 + (NP - P * j), width)]

        block = ctx.enter_context(nc.Block())

        @block.sync
        def _(sp):
            for dst, src in ((w0t, W0T.rearrange("(t p) k -> p t k", p=P)),
                             (a0_sb, a0.rearrange("(c p) h s -> p c h s", p=P)),
                             (w1t[0:FO], W1T), (a1_sb[0:FO], a1), (bi, ebi), (bh, ebh), (sel_sb[0:19], sel)):
                sp.dma_start(dst, src).then_inc(setup_loaded, 16)
            sp.dma_start(yT[:, :, :], xT.rearrange("(c p) n -> p c n", p=P)).then_inc(xT_loaded, 16)
            sp.dma_start(x_sb, x.rearrange("(t p) f -> p t f", p=P)).then_inc(x_loaded, 16)

            def load_tile(i0, j, width=IB):
                sp.dma_start(ring[:, j % RING, 0:width],
                             AT[P * j:P * (j + 1), ds(i0, width)]).then_inc(tile_loaded[j % RING], 16)

            def stream(used, blocks, width, extra):
                for j in range(RING):
                    load_tile(0, j, width)
                extra(0)
                with sp.Fori(0, blocks - 1) as b:
                    for j in range(RING, JT):
                        sp.wait_ge(used, b * JT + (j - RING + 1))
                        load_tile(b * width, j, width)
                    for j in range(RING):
                        sp.wait_ge(used, b * JT + (RING + j + 1))
                        load_tile((b + 1) * width, j, width)
                    extra(b + 1)
                for j in range(RING, JT):
                    sp.wait_ge(used, (blocks - 1) * JT + (j - RING + 1))
                    load_tile((blocks - 1) * width, j, width)

            sp.dma_start(gw[:, 0, :, :], eWi.rearrange("(c p) n -> p c n", p=P)).then_inc(egw_loaded, 16)
            sp.dma_start(gw[:, 1, :, :], eWh.rearrange("(c p) n -> p c n", p=P)).then_inc(egw_loaded, 16)

            def support_extra(b):
                if not (isinstance(b, int) and b == 0):
                    sp.wait_ge(G[0]["gru_done"], b * KC)
                sp.dma_start(diag1, diag[:, ds(b * IB, IB)].partition_broadcast(P).rearrange("p a n -> p (a n)")
                             ).then_inc(diag_loaded, 16)

            stream(support_in, NB, IB, support_extra)

            sp.wait_ge(e_ready, NB)
            sp.dma_start(e_dram, escore[0:NV, :]).then_inc(e_stored, 16)
            sp.wait_ge(e_stored, 16)
            sp.wait_ge(ecol_mm, 1)
            sp.wait_ge(flag_ready, 1)
            sp.wait_ge(support_mm, NB * JT)
            sp.wait_ge(G[0]["gru_done"], NB * KC)
            sp.dma_start(ebc, e_dram.partition_broadcast(P)).then_inc(ebc_loaded, 16)
            for k in range(2):
                sp.dma_start(a2[:, k, :], A[k * P:(k + 1) * P, :]).then_inc(a2_loaded[k], 16)
            with sp.Fori(0, JT // 2 - 1) as t:
                for k in range(2):
                    sp.wait_ge(rowmax_done, 2 * t + (k + 1))
                    sp.dma_start(a2[:, k, :], A[ds((2 * t + (2 + k)) * P, P), :]).then_inc(a2_loaded[k], 16)

            sp.wait_ge(rowmax_done, JT)
            sp.dma_start(xt2, xT.rearrange("(c p) n -> p c n", p=P)).then_inc(xt2_loaded, 16)
            sp.dma_start(w0, W0.rearrange("(c p) n -> p c n", p=P)).then_inc(xt2_loaded, 16)
            for dst, src in ((gw[:, 0, :, :], nWi.rearrange("(c p) n -> p c n", p=P)),
                             (gw[:, 1, :, :], nWh.rearrange("(c p) n -> p c n", p=P)), (bi, nbi), (bh, nbh)):
                sp.dma_start(dst, src).then_inc(ngw_loaded, 16)
            sp.wait_ge(nmT_ready, 1)
            sp.dma_start(nm_dram.rearrange("h (t p) -> (h t) p", p=P), nmT[0:HEADS * JT, :]).then_inc(nm_stored, 16)
            sp.wait_ge(nm_stored, 16)
            sp.wait_ge(hw_mm, 2 * JT)

            def attend_extra(b):
                first = isinstance(b, int) and b == 0
                if not first:
                    sp.wait_ge(arg_ready, b * JT * HEADS)
                sp.dma_start(negm, nm_dram[:, ds(b * IB, IB)].partition_broadcast(P)).then_inc(negm_loaded, 16)
                if not first:
                    sp.wait_ge(G[1]["gru_done"], b * KC)
                sp.dma_start(diag3, diag[:, ds(b * IB, IB)].partition_broadcast(P).rearrange("p a n -> p (a n)")
                             ).then_inc(xTb_loaded, 16)
                sp.dma_start(xTb, xT.rearrange("(c p) n -> p c n", p=P)[:, :, ds(b * IB, IB)]).then_inc(xTb_loaded, 16)

            stream(u_ready, NB, IB, attend_extra)

            sp.wait_ge(G[1]["gate_mm"], NB * KC * 4)
            sp.dma_start(wall[:, :, 0:H], W1.rearrange("(c p) n -> p c n", p=P)).then_inc(wall_loaded, 16)
            sp.wait_ge(strow_ready, JT)
            sp.dma_start(s_dram, strow[0:H1, :]).then_inc(s_stored, 16)
            sp.wait_ge(tmax_ready, 1)
            sp.dma_start(t_dram.rearrange("a h -> h a"), tmax[0:2 * H1, :]).then_inc(s_stored, 16)
            sp.wait_ge(s_stored, 32)
            sp.dma_start(tb, t_dram.partition_broadcast(P).rearrange("p a n -> p (a n)")).then_inc(tb_loaded, 16)

            def gat_extra(b):
                if not (isinstance(b, int) and b == 0):
                    sp.wait_ge(sg_ready, b * JT)
                sp.dma_start(sbc, s_dram[:, ds(b * IB1, IB1)].partition_broadcast(P)).then_inc(sbc_loaded, 16)

            sp.wait_ge(parts_ready, JT)
            stream(mask_ready, NB1, IB1, gat_extra)
            sp.wait_ge(o_stored, 16 * NB1)

        def pe_gru(pe, S, b, inT, hT, weights):
            for c in range(KC):
                q = b * KC + c

                def gate(dst, m, sources):
                    terms = [(s, kc) for s in sources for kc in range(KC)]
                    for n, (s, kc) in enumerate(terms):
                        mm = pe.matmul(dst[:, 0:IB], weights[:, s, kc, m * P:(m + 1) * P], (inT, hT)[s](kc),
                                       start=(n == 0), stop=(n == len(terms) - 1))
                    mm.then_inc(S["gate_mm"], 1)

                if c > 0:
                    pe.wait_ge(S["hn_read"], q)
                gate(bank[6], c, (0, 1))
                if c > 0:
                    pe.wait_ge(S["pre_ready"], q)
                gate(bank[7], KC + c, (0, 1))
                pe.wait_ge(S["r_read"], q + 1)
                gate(bank[6], 2 * KC + c, (1,))
                pe.wait_ge(S["z_read"], q + 1)
                gate(bank[7], 2 * KC + c, (0,))
            pe.wait_ge(S["hn_read"], b * KC + KC)
            pe.wait_ge(S["pre_ready"], b * KC + KC)

        def act_gru(act, S, b, buf):
            tr, tz, hq, nn, _, _ = buf
            for c in range(KC):
                q = b * KC + c
                if c > 0:
                    act.wait_ge(S["out_ready"], q)
                act.wait_ge(S["gate_mm"], 4 * q + 1)
                act.activation(tr, bank[6][:, 0:IB], ACT.Tanh, bias=brz[:, c:c + 1], scale=0.5).then_inc(S["r_read"], 1)
                act.wait_ge(S["gate_mm"], 4 * q + 2)
                act.activation(tz, bank[7][:, 0:IB], ACT.Tanh, bias=brz[:, KC + c:KC + c + 1],
                               scale=0.5).then_inc(S["z_read"], 1)
                act.wait_ge(S["gate_mm"], 4 * q + 3)
                act.activation(hq, bank[6][:, 0:IB], ACT.Identity, bias=bh[:, 4 + c:5 + c]).then_inc(S["hn_read"], 1)
                act.wait_ge(S["pre_ready"], q + 1)
                act.activation(nn, hq, ACT.Tanh, bias=bi[:, 4 + c:5 + c]).then_inc(S["n_ready"], 1)
            act.wait_ge(S["out_ready"], b * KC + KC)

        GRU_LINKS = 4 * KC

        def vec_gru(dve, S, b, buf, xin, dg, chain):
            tr, tz, hq, nn = buf[:4]
            for c in range(KC):
                q, dx = b * KC + c, buf[4 + c]
                dve.wait_ge(S["hn_read"], q + 1)
                chain.link(dve.scalar_tensor_tensor(hq, tr, 1.0, hq, ALU.add, ALU.mult))
                dve.wait_ge(S["gate_mm"], 4 * q + 4)
                dve.scalar_tensor_tensor(hq, hq, 0.5, bank[7][:, 0:IB], ALU.mult, ALU.add).then_inc(S["pre_ready"], 1)
                dve.wait_ge(S["n_ready"], q + 1)
                chain.link(dve.tensor_tensor(dx, xin(c), nn, ALU.subtract))
                chain.link(dve.scalar_tensor_tensor(dx, tz, 1.0, dx, ALU.add, ALU.mult))
                ins = dve.scalar_tensor_tensor(dx, dx, 0.5, nn, ALU.mult, ALU.add)
                ins.then_inc(S["out_ready"], 1)
                dve.wait_ge(S["out_ready"], q + 1)
                chain.link(dve.tensor_tensor(dx, dx, dg, ALU.mult))
            dve.wait_ge(S["gate_mm"], b * (4 * KC) + 4 * KC)
            for c in range(KC):
                y = yT[:, c, ds(b * IB, IB)]
                dve.tensor_tensor(y, y, buf[4 + c], ALU.add).then_inc(S["gru_done"], 1)

        @block.tensor
        def _(pe):
            pe.wait_ge(setup_loaded, 16 * 7)
            for h in range(HEADS):
                for kc in range(KC):
                    for oc in range(KC):
                        pe.matmul(bank[0][:, kc * NV + 2 * h:kc * NV + 2 * h + 2],
                                  w0t[:, h * KC + oc, kc * P:(kc + 1) * P], a0_sb[:, oc, h, :],
                                  start=(oc == 0), stop=(oc == KC - 1))
            for h in range(H1):
                for kc in range(KC):
                    o = kc * 2 * H1 + 2 * h
                    mm = pe.matmul(bank[1][:, o:o + 2], w1t[0:FO, h, kc * P:(kc + 1) * P], a1_sb[0:FO, h, :],
                                   start=True, stop=True)
            mm.then_inc(wa_done, 1)
            pe.wait_ge(wa_ready, 1)
            pe.wait_ge(xT_loaded, 16)
            for t in range(JT):
                for kc in range(KC):
                    mm = pe.matmul(bank[2][:, t * NV:(t + 1) * NV], yT[:, kc, t * P:(t + 1) * P], wa[:, kc, :],
                                   start=(kc == 0), stop=(kc == KC - 1))
            mm.then_inc(u_done, 1)

            pe.wait_ge(upar_ready, 1)
            pe.wait_ge(x_loaded, 16)
            pe.wait_ge(egw_loaded, 32)
            with pe.Fori(0, NB) as b:
                for j in range(JT):
                    pe.wait_ge(support_in, b * JT + (j + 1))
                    first, last = j == 0, j == JT - 1
                    for c in range(KC):
                        pe.matmul(bank[c][:, 0:IB], x_sb[:, j, c * P:(c + 1) * P], am[:, j % 2, :], start=first, stop=last)
                    pe.matmul(bank[2][0:19, 0:IB], upar[:, j, 0:19], pos[:, j % 2, :], start=first, stop=last)
                    pe.matmul(bank[3][0:19, 0:IB], upar[:, j, 0:19], neg[:, j % 2, :], start=first,
                              stop=last).then_inc(support_mm, 1)
                pe.wait_ge(support_evac, 4 * b + 4)
                pe.matmul(bank[4][0:CNT + 1, 0:IB], sel_sb[0:19, 0, :], usum[0:19, 0, :], start=True, stop=False)
                pe.matmul(bank[4][0:CNT + 1, 0:IB], sel_sb[0:19, 1, :], usum[0:19, 1, :], start=False,
                          stop=True).then_inc(sel_done, 1)
                pe_gru(pe, G[0], b, lambda kc: nsT[:, kc, :], lambda kc: yT[:, kc, ds(b * IB, IB)], gw)
                pe.wait_ge(zs_ready, b + 1)

            pe.wait_ge(e_ready, NB)
            for t in range(JT):
                mm = pe.transpose(bank[5][:, t * NV:(t + 1) * NV], escore[0:NV, t * P:(t + 1) * P], ident[0:NV, 0:NV])
            mm.then_inc(ecol_mm, 1)
            pe.wait_ge(nm_ready, 1)
            pe.transpose(bank[4][0:HEADS * JT, 0:P], nm, ident[:, :]).then_inc(nm_mm, 1)

            pe.wait_ge(xt2_loaded, 32)
            pe.wait_ge(ecol_ready, 1)
            pe.wait_ge(nmT_ready, 1)
            half = HEADS * H // 2
            for t in range(JT):
                for n in range(2):
                    if t >= 4:
                        pe.wait_ge((hw_evac_a, hw_evac_v)[n], t - 3)
                    for kc in range(KC):
                        mm = pe.matmul(bank[(2 * t + n) % 8][:, 0:half], xt2[:, kc, t * P:(t + 1) * P],
                                       w0[:, kc, n * half:(n + 1) * half], start=(kc == 0), stop=(kc == KC - 1))
                    mm.then_inc(hw_mm, 1)

            pe.wait_ge(hw_evac_a, JT)
            pe.wait_ge(hw_evac_v, JT)
            pe.wait_ge(ngw_loaded, 64)
            with pe.Fori(0, NB) as b:
                for j in range(JT):
                    pe.wait_ge(u_ready, b * JT + (j + 1))
                    for h in range(HEADS):
                        for c in range(KC):
                            mm = pe.matmul(bank[KC * h + c][:, 0:IB], hw[:, j, h * H + c * P:h * H + (c + 1) * P],
                                           u[:, j % 2, h, :], start=(j == 0), stop=(j == JT - 1))
                    mm.then_inc(attend_mm, 1)
                pe.wait_ge(wacc_ready, JT * b + JT)
                for h in range(HEADS):
                    if h == 2:
                        pe.wait_ge(den_read, HEADS * b + 1)
                    pe.matmul(bank[6 + h % 2][:, 0:IB], ones[:, :], wacc[:, h, :], start=True, stop=True).then_inc(den_mm, 1)
                pe.wait_ge(es_ready, b + 1)
                pe.wait_ge(xTb_loaded, 32 * b + 32)
                pe_gru(pe, G[1], b, lambda kc: esT[:, kc, :], lambda kc: xTb[:, kc, :], gw)

            pe.wait_ge(wall_loaded, 16)
            pe.wait_ge(bias_ready, 3)
            with pe.Fori(0, JT // 2) as tt:
                for k in range(2):
                    pe.wait_ge(ys_ready, 2 * tt + (k + 1))
                    for c in range(KC):
                        mm = pe.transpose(bank[k][:, c * P:(c + 1) * P], ys[:, k, c, :], ident[:, :])
                    mm.then_inc(yt_mm, 1)
                for k in range(2):
                    pe.wait_ge(xs_ready, 2 * tt + (k + 1))
                    for c in range(KC):
                        mm = pe.transpose(bank[2 + k][:, c * P:(c + 1) * P], xs[:, k, c * P:(c + 1) * P], ident[:, :])
                    mm.then_inc(x1T_mm, 1)
                for k in range(2):
                    pe.wait_ge(x1T_ready, 2 * tt + (k + 1))
                    for c in range(KC):
                        pe.matmul(bank[4 + k][:, 0:H + 2 * H1], x1T[:, k, c, :], wall[:, c, :], start=(c == 0), stop=(c == KC - 1))
                    for c in range(KC):
                        mm = pe.matmul(bank[6 + k][0:2 * H1, 0:P], wa1[:, c, :], x1T[:, k, c, :], start=(c == 0), stop=(c == KC - 1))
                    mm.then_inc(wh_mm, 1)
                pe.wait_ge(strow_ready, 2 * tt + 2)
                pe.wait_ge(wh_ready, 2 * tt + 2)

            def gat(b):
                first_block = isinstance(b, int)
                for j in range(JT):
                    pe.wait_ge(g_ready, b * JT + (j + 1))
                    for c in range(IT1):
                        for h in range(H1):
                            n = c * H1 + h
                            if j == 0 and not first_block:
                                pe.wait_ge(ev_ready, b * (IT1 * H1) + (n + 1 - IT1 * H1))
                            for q in range(2):
                                mm = pe.matmul(bank[n][:, q * PW:(q + 1) * PW], g[:, j % 2, q, h, c * P:(c + 1) * P],
                                               parts[:, j, h, q, :, :].rearrange("p a b -> p (a b)"),
                                               start=(j == 0 and q == 0), stop=(j == JT - 1), skip_group_check=True)
                    mm.then_inc(gat_mm, 1)

            pe.wait_ge(parts_ready, JT)
            gat(0)
            with pe.Fori(1, NB1) as b:
                gat(b)

        @block.gpsimd
        def _(pool):
            def one(shape):
                v = ones[:, 0:1]
                return (v if len(shape) == 1 else v.unsqueeze(1)).to_broadcast([P] + shape)

            pool.memset(offdiag[:, :], 1.0).then_inc(pool_chain, 1)
            pool.memset(ident[:, :], 0.0).then_inc(pool_chain, 1)
            pool.memset(zdiag[:, :], 0.0).then_inc(pool_chain, 1)
            pool.memset(ones[:, :], 1.0).then_inc(const_ready, 1)
            pool.memset(eps, EPS).then_inc(const_ready, 1)
            pool.wait_ge(pool_chain, 3)
            for v, fill in ((ident, 1.0), (zdiag, -BIG)):
                pool.affine_select(out=v[:, :], in_=v[:, :], compare_op=ALU.not_equal, fill=fill, base=0,
                                   pattern=[[-1, P]], channel_multiplier=1).then_inc(const_ready, 1)
            mid = offdiag[:, NP:NP + P]
            pool.affine_select(out=mid, in_=mid, compare_op=ALU.not_equal, fill=0.0, base=0,
                               pattern=[[-1, P]], channel_multiplier=1).then_inc(const_ready, 1)

            with pool.Fori(0, NB) as b:
                for j in range(JT):
                    pool.wait_ge(wgt_ready, (b * JT + (j + 1)) * HEADS)
                    if j == 0:
                        ins = pool.tensor_tensor(wacc, wgt[:, j % 2], one([HEADS, IB]), ALU.mult)
                    else:
                        pool.wait_ge(wacc_ready, b * JT + j)
                        ins = pool.tensor_tensor(wacc, wacc, wgt[:, j % 2], ALU.add)
                    ins.then_inc(wacc_ready, 1)
                pool.wait_ge(den_mm, b * HEADS + HEADS)

            with pool.Fori(0, JT // 2) as tt:
                for k in range(2):
                    t = 2 * tt + k
                    pool.wait_ge(xs_ready, t + 1)
                    pool.tensor_tensor(x1[:, t, :], xs[:, k, :], one([H]), ALU.mult).then_inc(x1_stored, 1)

            pool.wait_ge(coef_ready, 4)
            pool.wait_ge(x1_stored, JT)

            def gat_out(p):
                for c in range(IT1):
                    t = IT1 * p + c
                    pool.wait_ge(ev_ready, H1 * t + H1)
                    e = ev[:, c].rearrange("p h (q s o) -> p (h q) s o", q=2, s=3)
                    xq = xsum.rearrange("p h q o -> p (h q) o")
                    a_pos = acoef[:, 0, ds(t, 1), :].rearrange("p a h -> p h a").to_broadcast([P, H1, FP])
                    a_neg = acoef[:, 1, ds(t, 1), :].rearrange("p a h -> p h a").to_broadcast([P, H1, FP])
                    cnt = Count(pool, num_chain)
                    cnt.at(6 * t)
                    cnt.link(pool.tensor_tensor(xq, e[:, :, 1, :], e[:, :, 2, :], ALU.add))
                    cnt.link(pool.tensor_tensor(xq, xq, e[:, :, 0, :], ALU.add))
                    cnt.link(pool.tensor_tensor(tmp5, xsum[:, :, 0, :], a_pos, ALU.mult))
                    cnt.link(pool.tensor_tensor(num, xsum[:, :, 1, :], a_neg, ALU.mult))
                    cnt.link(pool.tensor_tensor(num, num, tmp5, ALU.add))
                    pool.sem_inc(num_ready, 1)
                    pool.wait_ge(rd_ready, t + 1)
                    y = y5[:, c, :]
                    cnt.link(pool.tensor_tensor(y.rearrange("p (h o) -> p h o", h=H1), num[:, :, 0:FO],
                                                rd1.unsqueeze(2).to_broadcast([P, H1, FO]), ALU.mult))
                    assert cnt.k == 6
                    pool.tensor_tensor(y, y, x1[:, t, :], ALU.add).then_inc(y_ready, 1)
                pool.wait_ge(o_ready, IT1 * p + IT1)

            with pool.Fori(0, NB1) as p:
                gat_out(p)

        @block.scalar
        def _(act):
            act.wait_ge(bias_ready, 1)
            with act.Fori(0, NB) as b:
                act.wait_ge(support_mm, b * JT + JT)
                for n in range(2):
                    act.copy(usum[0:19, n, :], bank[2 + n][0:19, 0:IB]).then_inc(support_evac, 1)
                for c in range(KC):
                    act.copy(nsT[:, c, :], bank[c][:, 0:IB]).then_inc(support_evac, 1)
                act.wait_ge(sel_done, b + 1)
                act.copy(zs[0:CNT + 1, :], bank[4][0:CNT + 1, 0:IB]).then_inc(zs_ready, 1)
                act_gru(act, G[0], b, gru1)
                act.wait_ge(e_ready, b + 1)

            half = HEADS * H // 2
            act.wait_ge(rowmax_done, JT)
            for t in range(JT):
                act.wait_ge(hw_mm, 2 * t + 1)
                act.copy(hw[:, t, 0:half], bank[(2 * t) % 8][:, 0:half]).then_inc(hw_evac_a, 1)

            act.wait_ge(bias_ready, 2)
            with act.Fori(0, NB) as b:
                for j in range(JT):
                    for h in range(HEADS):
                        act.wait_ge(arg_ready, (b * JT + j) * HEADS + (h + 1))
                        act.activation(wgt[:, j % 2, h, :], wgt[:, j % 2, h, :], ACT.Exp).then_inc(wgt_ready, 1)
                act_gru(act, G[1], b, gru3)

            act.wait_ge(G[1]["gru_done"], NB * KC)
            act.wait_ge(const_ready, 5)
            with act.Fori(0, JT // 2) as tt:
                for k in range(2):
                    act.copy(ys[:, k, :, :], yT[:, :, ds((2 * tt + k) * P, P)]).then_inc(ys_ready, 1)
                for k in range(2):
                    act.wait_ge(var_ready, 2 * tt + (k + 1))
                    act.activation(sd[:, k, :], mv[:, k, 1:2], ACT.Sqrt, bias=eps).then_inc(sd_ready, 1)
                for k in range(2):
                    act.wait_ge(x1T_mm, 2 * tt + (k + 1))
                    act.copy(x1T[:, k, :, :].rearrange("p c n -> p (c n)"), bank[2 + k][:, 0:H]).then_inc(x1T_ready, 1)
                for k in range(2):
                    t = 2 * tt + k
                    act.wait_ge(wh_mm, t + 1)
                    act.copy(wh[:, t, :], bank[4 + k][:, 0:H])
                    act.copy(st[:, t, :], bank[4 + k][:, H:H + 2 * H1]).then_inc(wh_ready, 1)

            act.wait_ge(ush_ready, 3)
            act.activation(bcoef[:, :, :, 0], ush, ACT.Exp).then_inc(coef_ready, 1)
            act.activation(bcoef[:, :, :, 1], ush, ACT.Exp, scale=SLOPE).then_inc(coef_ready, 1)
            act.activation(acoef[:, 0, :, :], acoef[:, 0, :, :], ACT.Exp, scale=1 - SLOPE).then_inc(coef_ready, 1)
            act.activation(acoef[:, 1, :, :], acoef[:, 1, :, :], ACT.Exp, scale=SLOPE - 1).then_inc(coef_ready, 1)

            act.wait_ge(s_stored, 32)
            with act.Fori(0, JT // 2) as tt:
                def part(k, i):
                    return parts[:, 2 * tt + k, :, :, i, :].rearrange("p h q o -> p (h q) o")

                def f(k):
                    return fx[:, k].rearrange("p h q o -> p (h q) o")

                for i, ready in enumerate((fx_ready, hi_ready, mid_ready)):
                    for k in range(2):
                        act.wait_ge(ready, 2 * tt + (k + 1))
                        act.copy(part(k, i), f(k)).then_inc((hi_cast, mid_cast, parts_ready)[i], 1)

            def gat(b, p):
                first_block = isinstance(b, int)
                act.wait_ge(sbc_loaded, b * 16 + 16)
                for j in range(JT):
                    if j >= 2 or not first_block:
                        act.wait_ge(pos_ready, b * JT + (j - 1))
                    for h in range(H1):
                        ins = act.activation(sg[:, j % 2, h, :], sbc[:, h, :], ACT.Sigmoid, bias=tsteep[:, j, h:h + 1],
                                             scale=STEEP)
                    ins.then_inc(sg_ready, 1)
                    if p is None:
                        continue
                    if j == 1:
                        gat_evac(p)
                    if j == 17:
                        gat_sqrt(p)
                    if j == 20:
                        gat_store(p)

            def gat_evac(p):
                act.wait_ge(gat_mm, p * JT + JT)
                for c in range(IT1):
                    for h in range(H1):
                        act.copy(ev[:, c, h, :], bank[c * H1 + h][:, 0:2 * PW]).then_inc(ev_ready, 1)

            def gat_sqrt(p):
                act.wait_ge(var5, p * IT1 + IT1)
                act.activation(sd5, mv5[:, :, 1], ACT.Sqrt, bias=eps).then_inc(sd5_ready, 1)

            def gat_store(p):
                act.wait_ge(o_ready, p * IT1 + IT1)
                act.dma_start(out[ds(p * IB1, IB1), :].rearrange("(c p) f -> p c f", p=P), o5).then_inc(o_stored, 16)

            gat(0, None)
            with act.Fori(1, NB1) as b:
                gat(b, b - 1)
            for last in (gat_evac, gat_sqrt, gat_store):
                last(NB1 - 1)

        @block.vector
        def _(dve):
            chain = Count(dve, vec_chain)
            dve.wait_ge(wa_done, 1)
            chain.link(dve.tensor_copy(wa1[:, :, :].rearrange("p c (s h) -> p c s h", s=2),
                                       bank[1][:, 0:4 * H1].rearrange("p (c h s) -> p c s h", c=KC, s=2)))
            dve.tensor_copy(wa, bank[0][:, 0:KC * NV].rearrange("p (c v) -> p c v", c=KC)).then_inc(wa_ready, 1)
            dve.wait_ge(setup_loaded, 16 * 7)
            chain.link(dve.tensor_tensor(brz, bi[:, 0:4], bh[:, 0:4], ALU.add))
            dve.tensor_scalar(brz, brz, 0.5, None, ALU.mult).then_inc(bias_ready, 1)
            dve.wait_ge(u_done, 1)
            chain.link(dve.tensor_copy(u_sb, bank[2][:, 0:JT * NV].rearrange("p (t v) -> p t v", v=NV)))
            chain.link(dve.memset(upar[:, :, 18:20], 1.0))
            chain.link(dve.tensor_copy(upar[:, :, 0:NV], u_sb))
            chain.link(dve.tensor_tensor(u_r, u_sb, upar[:, :, 0:NV], ALU.subtract))
            chain.link(dve.tensor_copy(upar[:, :, NV:2 * NV], u_r))
            chain.link(dve.tensor_tensor(u_r, u_r, upar[:, :, NV:2 * NV], ALU.subtract))
            dve.tensor_copy(upar[:, :, 2 * NV:3 * NV], u_r).then_inc(upar_ready, 1)

            dve.wait_ge(const_ready, 5)
            dve.wait_ge(xT_loaded, 16)
            loop = Count(dve, support_chain)
            with dve.Fori(0, NB) as b:
                loop.at(b * (JT + GRU_LINKS))
                for j in range(JT):
                    dve.wait_ge(tile_loaded[j % RING], 16 * (HALF * b + (j // RING + 1)))
                    if j >= 2:
                        dve.wait_ge(support_mm, b * JT + (j - 1))
                    loop.link(dve.tensor_tensor(am[:, j % 2, :], ring[:, j % RING, :], window(j, b * IB, IB), ALU.mult))
                    dve.tensor_scalar(pos[:, j % 2, :], am[:, j % 2, :], 0.0, None, ALU.is_gt)
                    dve.tensor_scalar(neg[:, j % 2, :], am[:, j % 2, :], 0.0, None, ALU.is_lt).then_inc(support_in, 1)
                dve.wait_ge(zs_ready, b + 1)
                dve.scalar_tensor_tensor(escore[0:CNT + 1, ds(b * IB, IB)], zs[0:CNT + 1, :], SLOPE, zs[0:CNT + 1, :],
                                         ALU.mult, ALU.max).then_inc(e_ready, 1)
                dve.wait_ge(diag_loaded, 16 * (b + 1))
                vec_gru(dve, G[0], b, gru1, lambda c: yT[:, c, ds(b * IB, IB)], diag1, loop)
                assert loop.k == JT + GRU_LINKS

            dve.wait_ge(e_ready, NB)
            chain.link(dve.tensor_reduce(flag[CNT:CNT + 1, :], escore[CNT:CNT + 1, :], AX.X, ALU.max))
            dve.tensor_copy(flag_i[CNT:CNT + 1, :], flag[CNT:CNT + 1, :]).then_inc(flag_ready, 1)
            dve.wait_ge(ecol_mm, 1)
            dve.tensor_copy(ecol, bank[5][:, 0:JT * NV].rearrange("p (t v) -> p t v", v=NV)).then_inc(ecol_ready, 1)
            dve.wait_ge(flag_ready, 1)
            negatives = dve.value_load(flag_i[CNT:CNT + 1, 0:1], min_val=0, max_val=NP)

            dve.wait_ge(ebc_loaded, 16)

            def rowmax(signed):
                loop = Count(dve, rowmax_chain[signed])
                with dve.Fori(0, JT // 2) as tt:
                    loop.at(tt * (10 * (1 + signed)))
                    for k in range(2):
                        t = 2 * tt + k
                        dve.wait_ge(a2_loaded[k], 16 * (tt + 1))
                        own = pen2[:, ds(t * P, P)]
                        for sign, (op, first) in enumerate(((ALU.is_le, 0), (ALU.is_ge, HEADS))[:1 + signed]):
                            loop.link(dve.tensor_scalar(pen2, a2[:, k, :], 0.0, -BIG, op, ALU.mult))
                            loop.settle(dve.tensor_tensor(own, own, zdiag[:, :], ALU.min), cell)
                            for h in range(HEADS):
                                ins = dve.tensor_tensor_reduce(junk, ebc[:, first + h, :], pen2, 1.0, -3.0e38,
                                                               ALU.add, ALU.max, mrow[:, sign, h:h + 1])
                                loop.settle(ins, cell)
                        m = mcol[:, ds(t, 1), :].rearrange("p a h -> p (a h)")
                        if signed:
                            dve.tensor_tensor(m, mrow[:, 0, :], mrow[:, 1, :], ALU.max).then_inc(rowmax_done, 1)
                        else:
                            dve.tensor_copy(m, mrow[:, 0, :]).then_inc(rowmax_done, 1)
                    used = loop.k
                assert used == 10 * (1 + signed), used

            with dve.If(negatives > 0):
                rowmax(True)
            with dve.Else():
                rowmax(False)
            dve.wait_ge(rowmax_done, JT)
            dve.tensor_scalar(nm.rearrange("p (h t) -> p t h", h=HEADS), mcol, -1.0, None, ALU.mult).then_inc(nm_ready, 1)
            dve.wait_ge(nm_mm, 1)
            dve.tensor_copy(nmT[0:HEADS * JT, :], bank[4][0:HEADS * JT, 0:P]).then_inc(nmT_ready, 1)

            half = HEADS * H // 2
            for t in range(JT):
                dve.wait_ge(hw_mm, 2 * t + 2)
                dve.tensor_copy(hw[:, t, half:2 * half], bank[(2 * t + 1) % 8][:, 0:half]).then_inc(hw_evac_v, 1)
            dve.wait_ge(ngw_loaded, 64)
            chain.link(dve.tensor_tensor(brz, bi[:, 0:4], bh[:, 0:4], ALU.add))
            dve.tensor_scalar(brz, brz, 0.5, None, ALU.mult).then_inc(bias_ready, 1)

            dve.wait_ge(nm_stored, 16)
            DEN_LINKS = HEADS * (1 + KC) + (HEADS - 1) * KC - 1

            def attend(signed):
                loop = Count(dve, attend_chain[signed])
                STEP = 4 + 2 * HEADS if signed else 2

                def arguments(b, j):
                    s = j % 2
                    tile = ring[:, j % RING, :]
                    dve.wait_ge(tile_loaded[j % RING], 16 * (HALF * NB + HALF * b + (j // RING + 1)))
                    if j >= 2:
                        dve.wait_ge(wacc_ready, b * JT + (j - 1))
                    loop.link(dve.scalar_tensor_tensor(mask3, tile, 0.0, window(j, b * IB, IB), ALU.is_gt, ALU.mult))
                    loop.link(dve.tensor_scalar(pen3, mask3, -1.0, BIG, ALU.add, ALU.mult))
                    for h in range(HEADS):
                        ins = dve.scalar_tensor_tensor(wgt[:, s, h, :], negm[:, h, :], ecol[:, j, h:h + 1], pen3,
                                                       ALU.add, ALU.min)
                        if signed:
                            loop.link(ins)
                        else:
                            ins.then_inc(arg_ready, 1)
                    if not signed:
                        return
                    loop.link(dve.scalar_tensor_tensor(mask3, tile, 0.0, window(j, b * IB, IB), ALU.is_lt, ALU.mult))
                    loop.link(dve.tensor_scalar(pen3, mask3, -1.0, BIG, ALU.add, ALU.mult))
                    for h in range(HEADS):
                        if h > 0:
                            dve.wait_ge(arg_ready, (b * JT + j) * HEADS + h)
                        loop.link(dve.scalar_tensor_tensor(argn, negm[:, h, :], ecol[:, j, HEADS + h:HEADS + h + 1],
                                                           pen3, ALU.add, ALU.min))
                        dve.tensor_tensor(wgt[:, s, h, :], wgt[:, s, h, :], argn, ALU.max).then_inc(arg_ready, 1)

                def products(b, j):
                    s = j % 2
                    dve.wait_ge(wgt_ready, (b * JT + (j + 1)) * HEADS)
                    if j >= 2:
                        dve.wait_ge(attend_mm, b * JT + (j - 1))
                    dve.tensor_tensor(u[:, s, :, :], wgt[:, s, :, :],
                                      ring[:, j % RING, :].unsqueeze(1).to_broadcast([P, HEADS, IB]),
                                      ALU.mult).then_inc(u_ready, 1)

                with dve.Fori(0, NB) as b:
                    dve.wait_ge(negm_loaded, 16 * (b + 1))
                    loop.at(b * (STEP * JT + DEN_LINKS + GRU_LINKS))
                    for j in range(JT + 1):
                        if j < JT:
                            arguments(b, j)
                        if j > 0:
                            products(b, j - 1)
                    dve.wait_ge(attend_mm, b * JT + JT)
                    for h in range(HEADS):
                        dve.wait_ge(den_mm, b * HEADS + (h + 1))
                        dve.tensor_scalar(rden, bank[6 + h % 2][:, 0:IB], TINY, float(HEADS), ALU.max,
                                          ALU.mult).then_inc(den_read, 1)
                        dve.wait_ge(den_read, b * HEADS + (h + 1))
                        loop.link(dve.reciprocal(rden, rden))
                        for c in range(KC):
                            num3 = bank[KC * h + c][:, 0:IB]
                            if h == 0:
                                loop.link(dve.tensor_tensor(esT[:, c, :], num3, rden, ALU.mult))
                                continue
                            loop.link(dve.tensor_tensor(gru3[4], num3, rden, ALU.mult))
                            ins = dve.tensor_tensor(esT[:, c, :], esT[:, c, :], gru3[4], ALU.add)
                            if h == HEADS - 1 and c == KC - 1:
                                ins.then_inc(es_ready, 1)
                            else:
                                loop.link(ins)
                    dve.wait_ge(xTb_loaded, 32 * (b + 1))
                    vec_gru(dve, G[1], b, gru3, lambda c: xTb[:, c, :], diag3, loop)
                    used = loop.k
                assert used == STEP * JT + DEN_LINKS + GRU_LINKS, used - STEP * JT

            with dve.If(negatives > 0):
                attend(True)
            with dve.Else():
                attend(False)

            dve.wait_ge(G[1]["gate_mm"], NB * KC * 4)
            dve.tensor_copy(wall[:, :, H:H + 2 * H1], wa1[:, :, :]).then_inc(bias_ready, 1)
            chain.link(dve.tensor_scalar(offdiag[:, :], offdiag[:, :], -1.0, 1.0, ALU.mult, ALU.add))
            loop = Count(dve, norm_chain)
            with dve.Fori(0, JT // 2) as tt:
                loop.at(tt * 4)
                for k in range(2):
                    dve.wait_ge(yt_mm, 2 * tt + (k + 1))
                    loop.settle(dve.bn_stats(stats[:, k, :], bank[k][:, 0:H]), cell)
                    dve.bn_aggr(mv[:, k, :], stats[:, k, :]).then_inc(var_ready, 1)
                for k in range(2):
                    dve.wait_ge(sd_ready, 2 * tt + (k + 1))
                    loop.link(dve.reciprocal(rstd[:, k, :], sd[:, k, :]))
                    dve.tensor_scalar(xs[:, k, :], bank[k][:, 0:H], mv[:, k, 0:1], rstd[:, k, 0:1], ALU.subtract,
                                      ALU.mult).then_inc(xs_ready, 1)
                for k in range(2):
                    t = 2 * tt + k
                    dve.wait_ge(wh_mm, t + 1)
                    dve.tensor_copy(strow[0:2 * H1, ds(t * P, P)], bank[6 + k][0:2 * H1, 0:P]).then_inc(strow_ready, 1)
                dve.wait_ge(x1_stored, 2 * tt + 2)

            dve.wait_ge(strow_ready, JT)
            dve.tensor_reduce(tmax[0:2 * H1, :], strow[0:2 * H1, 0:N], AX.X, ALU.max).then_inc(tmax_ready, 1)
            dve.wait_ge(tb_loaded, 16)
            dve.wait_ge(wh_ready, JT)
            dve.wait_ge(ys_ready, JT)
            s_col, t_col = st[:, :, 0:H1], st[:, :, H1:2 * H1]
            t_top = tb[:, H1:2 * H1].unsqueeze(1).to_broadcast([P, JT, H1])
            chain.link(dve.tensor_tensor(ush, t_col, t_top, ALU.subtract))
            dve.tensor_scalar(ush, ush, 0.0, None, ALU.min).then_inc(ush_ready, 1)
            chain.link(dve.tensor_tensor(acoef[:, 1, :, :], s_col, t_top, ALU.add))
            chain.link(dve.tensor_scalar(acoef[:, 0, :, :], acoef[:, 1, :, :], 0.0, None, ALU.min))
            dve.tensor_scalar(acoef[:, 1, :, :], acoef[:, 1, :, :], 0.0, None, ALU.max).then_inc(ush_ready, 1)
            dve.tensor_scalar(tsteep, t_col, STEEP, None, ALU.mult).then_inc(ush_ready, 1)

            dve.wait_ge(coef_ready, 4)
            loop = Count(dve, parts_chain)
            with dve.Fori(0, JT // 2) as tt:
                loop.at(tt * 4)
                for k in range(2):
                    t = 2 * tt + k
                    for q in range(2):
                        loop.link(dve.tensor_tensor(fx[:, k, :, q, 0:FO], wh[:, t, :].rearrange("p (h o) -> p h o", h=H1),
                                                    bcoef[:, t, :, q:q + 1].to_broadcast([P, H1, FO]), ALU.mult))
                    dve.tensor_scalar(fx[:, k, :, :, FO:FP].rearrange("p h q o -> p h (q o)"),
                                      bcoef[:, ds(t, 1), :, :].rearrange("p a h q -> p (a h) q"), 1.0, None,
                                      ALU.mult).then_inc(fx_ready, 1)
                for cast, i, ready in ((hi_cast, 0, hi_ready), (mid_cast, 1, mid_ready)):
                    for k in range(2):
                        f = fx[:, k].rearrange("p h q o -> p (h q) o")
                        dve.wait_ge(cast, 2 * tt + (k + 1))
                        part = parts[:, 2 * tt + k, :, :, i, :].rearrange("p h q o -> p (h q) o")
                        dve.tensor_tensor(f, f, part, ALU.subtract).then_inc(ready, 1)
                dve.wait_ge(parts_ready, 2 * tt + 2)

            def gat_mask(b, j):
                first_block = isinstance(b, int)
                dve.wait_ge(tile_loaded[j % RING], 16 * (2 * HALF * NB + HALF * b + (j // RING + 1)))
                if j >= 2 or not first_block:
                    dve.wait_ge(g_ready, b * JT + (j - 1))
                dve.scalar_tensor_tensor(mask5[:, j % 2, :], ring[:, j % RING, 0:IB1], 0.0, window(j, b * IB1, IB1),
                                         ALU.not_equal, ALU.max).then_inc(mask_ready, 1)

            def gat(b, p):
                first_block = isinstance(b, int)
                gat_mask(b, 0)
                for j in range(JT):
                    s = j % 2
                    m = mask5[:, s, :].unsqueeze(1).to_broadcast([P, H1, IB1])
                    dve.wait_ge(mask_ready, b * JT + (j + 1))
                    dve.wait_ge(sg_ready, b * JT + (j + 1))
                    if j >= 2 or not first_block:
                        dve.wait_ge(gat_mm, b * JT + (j - 1))
                    dve.tensor_tensor(g[:, s, 0, :, :], sg[:, s, :, :], m, ALU.mult).then_inc(pos_ready, 1)
                    if j + 1 < JT:
                        gat_mask(b, j + 1)
                    dve.wait_ge(pos_ready, b * JT + (j + 1))
                    dve.tensor_tensor(g[:, s, 1, :, :], m, g[:, s, 0, :, :], ALU.subtract).then_inc(g_ready, 1)
                    if p is None:
                        continue
                    for c in range(IT1):
                        if j == 8 + 5 * c:
                            gat_reciprocal(p, c)
                        if j == 15 + c:
                            gat_moments(p, c)
                    if j == 18:
                        gat_norm(p)
                if p is not None:
                    dve.wait_ge(o_stored, p * 16 + 16)

            def gat_reciprocal(p, c):
                dve.wait_ge(num_ready, p * IT1 + (c + 1))
                dve.reciprocal(rd1, num[:, :, FO:FP].rearrange("p h o -> p (h o)")).then_inc(rd_ready, 1)

            def gat_moments(p, c):
                cnt = Count(dve, gat_chain)
                cnt.at(p * (IT1 + 1) + c)
                dve.wait_ge(y_ready, p * IT1 + (c + 1))
                cnt.settle(dve.bn_stats(stat5[:, c, :], y5[:, c, :]), cell)
                dve.bn_aggr(mv5[:, c, :], stat5[:, c, :]).then_inc(var5, 1)

            def gat_norm(p):
                cnt = Count(dve, gat_chain)
                cnt.at(p * (IT1 + 1) + IT1)
                dve.wait_ge(sd5_ready, p + 1)
                cnt.link(dve.reciprocal(rs5, sd5))
                for c in range(IT1):
                    dve.tensor_scalar(o5[:, c, :], y5[:, c, :], mv5[:, c, 0:1], rs5[:, c:c + 1], ALU.subtract,
                                      ALU.mult).then_inc(o_ready, 1)

            dve.wait_ge(parts_ready, JT)
            gat(0, None)
            with dve.Fori(1, NB1) as b:
                gat(b, b - 1)
            for c in range(IT1):
                gat_reciprocal(NB1 - 1, c)
                gat_moments(NB1 - 1, c)
            gat_norm(NB1 - 1)


def kernel(**inputs):
    import numpy as _np
    import concourse.bacc as _bacc
    from concourse import mybir as _mybir
    from concourse.bass_utils import run_bass_kernel_spmd as _run

    v = {k: _np.asarray(a) for k, a in inputs.items()}
    adj = _np.zeros((NP, NP), _np.float32)
    adj[:N, :N] = v["adj"]
    x = _np.zeros((NP, H), _np.float32)
    x[:N] = v["x"]
    diag = _np.zeros((1, NP), _np.float32)
    diag[0, :N] = v["adj"].diagonal()
    sel = _np.zeros((19, 2, CNT + 1), _np.float32)
    for part in range(3):
        for h in range(HEADS):
            first, second = part * NV + 2 * h, part * NV + 2 * h + 1
            sel[first, 0, h] = sel[second, 1, h] = 1.0
            sel[first, 1, HEADS + h] = sel[second, 0, HEADS + h] = 1.0
    sel[18, 1, CNT] = 1.0
    gat_W, gat_a = v["L0_gnn_gat_W"], v["L0_gnn_gat_a"]
    W1, a1 = v["L1_gnn_W"], v["L1_gnn_a"]

    def bias(b):
        return b.reshape(6, P).T

    arrays = {
        "A": adj, "AT": adj.T, "x": x, "xT": x.T, "diag": diag,
        "W0": gat_W.transpose(1, 0, 2).reshape(H, HEADS * H),
        "W0T": gat_W.transpose(0, 2, 1).reshape(HEADS * H, H),
        "a0": gat_a.reshape(HEADS, 2, H).transpose(2, 0, 1),
        "eWi": v["L0_gnn_edge_Wih"].T, "eWh": v["L0_gnn_edge_Whh"].T,
        "ebi": bias(v["L0_gnn_edge_bih"]), "ebh": bias(v["L0_gnn_edge_bhh"]),
        "nWi": v["L0_gnn_node_Wih"].T, "nWh": v["L0_gnn_node_Whh"].T,
        "nbi": bias(v["L0_gnn_node_bih"]), "nbh": bias(v["L0_gnn_node_bhh"]),
        "W1": W1.transpose(1, 0, 2).reshape(H, H), "W1T": W1.transpose(2, 0, 1),
        "a1": a1.reshape(H1, 2, FO).transpose(2, 0, 1), "sel": sel,
    }
    arrays = {k: _np.ascontiguousarray(a) for k, a in arrays.items()}
    nc = _bacc.Bacc("TRN2", target_bir_lowering=False, num_devices=1)
    args = [nc.dram_tensor(f"in_{k}", a.shape, _mybir.dt.from_np(a.dtype), kind="ExternalInput").ap()
            for k, a in arrays.items()]
    out = nc.dram_tensor("out", (NP, H), _mybir.dt.float32, kind="ExternalOutput").ap()
    build(nc, *args, out)
    r = _run(nc, [{f"in_{k}": a for k, a in arrays.items()}], core_ids=[0])
    return r.results[0]["out"][:N]
```

```python
from contextlib import ExitStack

import numpy as np

import concourse.bass as bass
from concourse import mybir

ALU = mybir.AluOpType
ACT = mybir.ActivationFunctionType
AX = mybir.AxisListType
F32 = mybir.dt.float32
BF16 = mybir.dt.bfloat16
I32 = mybir.dt.int32

P = 128
N = 3327
JT = -(-N // P)
NP = JT * P
H = 256
KC = H // P
HEADS = 3
NV = 2 * HEADS
IB = 416
NB = NP // IB
RING = 13
HALF = JT // RING
GATES = 3 * H
CHUNKS = [(JT * i // 4, JT * (i + 1) // 4) for i in range(4)]
CNT = 32
H1, FO = 4, 64
FP = FO + 1
IB1 = 256
NB1 = NP // IB1
IT1 = IB1 // P
STEPS = 4
TILES = 4
assert NB1 % 2 == 1 and 2 * JT % STEPS == 0
PW = 3 * FP
BIG = 1e30
TINY = 1e-30
STEEP = 1e30
SLOPE = 0.2
EPS = 1e-5


def ds(start, size):
    return bass.ds(start, size)


class Count:

    def __init__(self, eng, sem):
        self.eng, self.sem, self.base, self.k = eng, sem, 0, 0

    def at(self, base):
        self.base, self.k = base, 0

    def link(self, ins):
        self.k += 1
        ins.then_inc(self.sem, 1)
        self.eng.wait_ge(self.sem, self.base + self.k)

    def settle(self, ins, cell):
        self.link(ins)
        self.eng.memset(cell, 0.0)


def build(nc, A, AT, x, xT, diag, W0, W0T, a0, eWi, eWh, ebi, ebh, nWi, nWh, nbi, nbh, W1, W1T, a1, sel, out):
    e_dram = nc.dram_tensor("e_dram", (NV, NP), F32, kind="Internal").ap()
    nm_dram = nc.dram_tensor("nm_dram", (2 * HEADS, NP), F32, kind="Internal").ap()
    s_dram = nc.dram_tensor("s_dram", (H1, NP + IB1), F32, kind="Internal").ap()
    pen_dram = nc.dram_tensor("pen_dram", (NP, NP), BF16, kind="Internal").ap()
    t_dram = nc.dram_tensor("t_dram", (1, 2 * H1), F32, kind="Internal").ap()

    ctx = ExitStack()
    with ctx:
        def sb(name, shape, dt=F32):
            return ctx.enter_context(nc.sbuf_tensor(name, shape, dt))

        def sem(name):
            return ctx.enter_context(nc.semaphore(name))

        yT = sb("yT", [P, KC, NP])
        offdiag = sb("offdiag", [P, 2 * NP], BF16)
        ring = sb("ring", [P, RING, IB])
        gw = sb("gw", [P, 2, KC, GATES])
        ident = sb("ident", [P, P])
        zdiag = sb("zdiag", [P, P], BF16)
        small = sb("small", [P, 768])
        flag_i = sb("flag_i", [P, 1], I32)
        WORK = 33740
        work = sb("work", [P, WORK])

        def carve(tensor, limit):
            at = [0]

            def take(shape, dt=F32):
                n = int(np.prod(shape))
                words = n if dt == F32 else n // 2
                v = tensor[:, at[0]:at[0] + words]
                at[0] += words
                assert at[0] <= limit, (at[0], limit)
                if dt == BF16:
                    v = v.bitcast(BF16)
                names = "abcde"[:len(shape)]
                if len(shape) > 1:
                    v = v.rearrange("p (%s) -> p %s" % (" ".join(names), " ".join(names)),
                                    **{c: s for c, s in zip(names, shape)})
                return v
            take.at = at
            return take

        tk = carve(small, 768)
        a0_sb = tk([KC, HEADS, 2])
        wa = tk([KC, NV])
        a1_sb = tk([H1, 2])
        bi = tk([6])
        bh = tk([6])
        brz = tk([4])
        ecol = tk([JT, NV])
        ebias = tk([JT, HEADS])
        mcol = tk([JT, HEADS])
        dcol = tk([JT, HEADS])
        mrow = tk([2, HEADS])
        mneg = tk([2, HEADS])
        dsum = tk([2, HEADS])
        cell = tk([1])
        mbig = tk([1])
        flag = tk([1])
        stats = tk([2, 6])
        mv = tk([2, 2])
        sd = tk([2])
        rstd = tk([2])
        eps = tk([1])
        tmax = tk([1])
        tb = tk([2 * H1])
        st = tk([JT, 2 * H1])

        def gru_buffers(tk):
            return [tk([IB]) for _ in range(6)]

        tk = carve(work, WORK)
        x_sb = tk([JT, H])
        escore = tk([NP])
        nsT = tk([KC, IB])
        usum = tk([2, IB])
        zs = tk([IB])
        gru1 = gru_buffers(tk)
        diag1 = tk([IB])
        w0t = tk([HEADS * KC, H])
        w1t = tk([H1, H])
        u_sb = tk([JT, NV])
        u_r = tk([JT, NV])
        upar = tk([JT, 20], BF16)
        sel_sb = tk([2, CNT + 1])
        penw = tk([RING, IB], BF16)
        am = tk([RING, IB])
        pos = tk([RING, IB], BF16)
        neg = tk([RING, IB], BF16)

        tk = carve(work, WORK)
        ebc = tk([NV, NP])
        a2 = tk([2, NP])
        pen2 = tk([NP], BF16)
        args = [tk([NP]), ring[:, :, :].rearrange("p a b -> p (a b)")[:, 0:NP]]
        rdT = tk([P])
        nmT = tk([P])
        take_nm = carve(pen2.bitcast(F32), NP // 2)
        nm = take_nm([HEADS * JT])
        rd = take_nm([HEADS * JT])
        assert tk.at[0] <= WORK - KC * HEADS * H

        tk = carve(work, WORK)
        hw = tk([JT, HEADS * H])
        xt2 = tk([KC, NP])
        tk.at[0] = WORK - KC * HEADS * H
        w0 = tk([KC, HEADS * H])
        tk.at[0] = JT * HEADS * H
        wgt = tk([2, HEADS, IB])
        u = tk([2, HEADS, IB])
        rdr = tk([HEADS, IB])
        negm = tk([HEADS, IB])
        esT = tk([KC, IB])
        xTb = tk([KC, IB])
        diag3 = tk([IB])
        mask3 = tk([IB], BF16)
        pen3 = tk([IB], BF16)
        penr = tk([2, IB], BF16)
        term = tk([IB])
        argn = tk([IB])
        gru3 = gru_buffers(tk)
        nums = gru3

        tk = carve(work, WORK)
        x1 = tk([JT, H])
        early = tk.at[0]
        parts = tk([JT, H1, 2, 3, FP], BF16)
        spare = tk.at[0]
        wh = tk([JT, H])
        tk = carve(work, WORK)
        tk.at[0] = early
        strow = tk([NP])
        ys = tk([2, KC, P])
        xs = tk([2, H])
        x1T = tk([2, KC, P])
        tk = carve(work, WORK)
        tk.at[0] = spare
        g = tk([2, 2, H1, IB1], BF16)
        ev = tk([IT1, H1, 2 * PW])
        sbc1 = tk([H1, IB1])
        tky = carve(yT[:, :, :].rearrange("p a b -> p (a b)"), KC * NP)
        bcoef = tky([JT, H1, 2])
        acoef = tky([2, JT, H1])
        ush = tky([JT, H1])
        tsteep = tky([JT, H1])
        at_fx = tky.at[0]
        fx = tky([TILES, H1, 2, FP])
        end_fx = tky.at[0]
        tky.at[0] = at_fx
        xsum = tky([IT1 * H1, 2, FP])
        mask5 = tky([2, IB1], BF16)
        sbc = [tky([H1, IB1]), sbc1]
        tmp5 = tky([IT1 * H1, FP])
        num = tky([IT1 * H1, FP])
        rd1 = tky([IT1 * H1])
        y5 = tky([IT1, H])
        o5 = tky([IT1, H])
        stat5 = tky([IT1, 6])
        mv5 = tky([IT1, 2])
        sd5 = tky([IT1])
        rs5 = tky([IT1])
        tkw = carve(gw[:, :, :, :].rearrange("p a b c -> p (a b c)"), 2 * KC * GATES)
        wall = tkw([KC, H + 2 * H1])
        sg = tkw([STEPS, H1, IB1], BF16)
        wa1 = sb("wa1", [P, KC, 2 * H1])

        bank = [ctx.enter_context(nc.psum_tensor(f"bank{i}", [P, 512], F32)) for i in range(8)]

        const_ready, vec_chain, pool_chain = sem("const_ready"), sem("vec_chain"), sem("pool_chain")
        support_chain, norm_chain, parts_chain, gat_chain = [sem(n + "_chain") for n in ("support", "norm", "parts", "gat")]
        rowmax_chain = [sem("rowmax_chain"), sem("rowmax_chain_signed")]
        attend_chain = [sem("attend_chain"), sem("attend_chain_signed")]
        setup_loaded, xT_loaded, egw_loaded = sem("setup_loaded"), sem("xT_loaded"), sem("egw_loaded")
        x_loaded = [sem(f"x_loaded{i}") for i in range(len(CHUNKS))]
        wa_done, wa_ready, u_done, upar_ready = sem("wa_done"), sem("wa_ready"), sem("u_done"), sem("upar_ready")
        tile_loaded = [sem(f"tile_loaded{i}") for i in range(RING)]
        support_in, support_mm, support_evac = sem("support_in"), sem("support_mm"), sem("support_evac")
        sel_done, zs_ready, e_ready = sem("sel_done"), sem("zs_ready"), sem("e_ready")
        diag_loaded, bias_ready = sem("diag_loaded"), sem("bias_ready")
        G = [{k: sem(f"{k}_{p}") for k in ("gate_mm", "r_read", "z_read", "hn_read", "pre_ready", "n_ready", "out_ready", "gru_done")}
             for p in ("edge", "node")]
        e_stored, ebc_loaded = sem("e_stored"), [sem(f"ebc_loaded{i}") for i in range(HEADS + 1)]
        a2_loaded = [sem("a2_loaded0"), sem("a2_loaded1")]
        ecol_mm, ecol_ready, flag_ready, rowmax_done = sem("ecol_mm"), sem("ecol_ready"), sem("flag_ready"), sem("rowmax_done")
        nm_ready, nm_mm, nmT_ready, nm_stored = sem("nm_ready"), sem("nm_mm"), sem("nmT_ready"), sem("nm_stored")
        xt2_loaded, w0_loaded = [sem(f"xt2_loaded{i}") for i in range(len(CHUNKS))], sem("w0_loaded")
        hw_mm, hw_evac_a, hw_evac_v = sem("hw_mm"), sem("hw_evac_a"), sem("hw_evac_v")
        ngw_loaded, negm_loaded, xTb_loaded = sem("ngw_loaded"), sem("negm_loaded"), sem("xTb_loaded")
        arg_ready, wgt_ready, u_ready, attend_mm, ebias_ready = [sem(n) for n in ("arg_ready", "wgt_ready", "u_ready", "attend_mm", "ebias_ready")]
        num_evac, rd_loaded, es_ready = sem("num_evac"), sem("rd_loaded"), sem("es_ready")
        wall_loaded = sem("wall_loaded")
        ys_ready, yt_mm, var_ready, sd_ready, xs_ready, x1_stored, x1T_mm, x1T_ready, wh_mm, wh_ready, strow_ready = [
            sem(n) for n in ("ys_ready", "yt_mm", "var_ready", "sd_ready", "xs_ready", "x1_stored", "x1T_mm",
                             "x1T_ready", "wh_mm", "wh_ready", "strow_ready")]
        tmax_ready, s_stored, tb_loaded, ush_ready, coef_ready, fx_ready, parts_ready = [
            sem(n) for n in ("tmax_ready", "s_stored", "tb_loaded", "ush_ready", "coef_ready", "fx_ready", "parts_ready")]
        sbc_loaded = [sem("sbc_loaded0"), sem("sbc_loaded1")]
        sg_ready, mask_ready, pos_ready, g_ready, gat_mm, ev_ready, num_chain, num_ready, rd_ready, y_ready, \
            var5, sd5_ready, o_ready, o_stored = [
                sem(n) for n in ("sg_ready", "mask_ready", "pos_ready", "g_ready", "gat_mm", "ev_ready",
                                 "num_chain", "num_ready", "rd_ready", "y_ready", "var5", "sd5_ready", "o_ready",
                                 "o_stored")]
        pen_stored, pen_loaded = [sem(f"pen_stored{i}") for i in range(RING)], [sem("pen_loaded0"), sem("pen_loaded1")]
        max_ready, exp_done, den_ready = sem("max_ready"), sem("exp_done"), sem("den_ready")
        gru_chain, es_chain, out_chain = [sem("edge_chain"), sem("node_chain")], sem("es_chain"), sem("out_chain")
        hi_cast, mid_cast, hi_ready, mid_ready = [sem(n) for n in ("hi_cast", "mid_cast", "hi_ready", "mid_ready")]

        def window(j, i0, width):
            return offdiag[:, ds(i0 + (NP - P * j), width)]

        def sg_slot(odd, j):
            return (odd * JT + j) % STEPS

        block = ctx.enter_context(nc.Block())

        @block.sync
        def _(sp):
            for dst, src in ((w0t, W0T.rearrange("(t p) k -> p t k", p=P)),
                             (a0_sb, a0.rearrange("(c p) h s -> p c h s", p=P)),
                             (w1t[0:FO], W1T), (a1_sb[0:FO], a1), (bi, ebi), (bh, ebh), (sel_sb[0:19], sel)):
                sp.dma_start(dst, src).then_inc(setup_loaded, 16)
            sp.dma_start(yT[:, :, :], xT.rearrange("(c p) n -> p c n", p=P)).then_inc(xT_loaded, 16)

            def load_tile(i0, j, width=IB):
                sp.dma_start(ring[:, j % RING, 0:width],
                             AT[P * j:P * (j + 1), ds(i0, width)]).then_inc(tile_loaded[j % RING], 16)

            def stream(used, blocks, width, head):
                head(0)
                with sp.Fori(0, blocks - 1) as b:
                    for j in range(RING, JT):
                        sp.wait_ge(used, b * JT + (j - RING + 1))
                        load_tile(b * width, j, width)
                    for j in range(RING):
                        sp.wait_ge(used, b * JT + (RING + j + 1))
                        load_tile((b + 1) * width, j, width)
                    head(b + 1)
                for j in range(RING, JT):
                    sp.wait_ge(used, (blocks - 1) * JT + (j - RING + 1))
                    load_tile((blocks - 1) * width, j, width)

            for i, (t0, t1) in enumerate(CHUNKS):
                sp.dma_start(x_sb[:, t0:t1, :], x[t0 * P:t1 * P, :].rearrange("(t p) f -> p t f", p=P)
                             ).then_inc(x_loaded[i], 16)
                for j in range(RING * i // len(CHUNKS), RING * (i + 1) // len(CHUNKS)):
                    load_tile(0, j)
            sp.dma_start(gw[:, 0, :, :], eWi.rearrange("(c p) n -> p c n", p=P)).then_inc(egw_loaded, 16)
            sp.dma_start(gw[:, 1, :, :], eWh.rearrange("(c p) n -> p c n", p=P)).then_inc(egw_loaded, 16)
            stream(support_in, NB, IB, lambda b: None)

            sp.wait_ge(e_ready, NB)
            sp.dma_start(e_dram, escore[0:NV, :]).then_inc(e_stored, 16)
            sp.wait_ge(e_stored, 16)
            sp.wait_ge(ecol_mm, 1)
            sp.wait_ge(flag_ready, 1)
            sp.wait_ge(support_mm, NB * JT)
            for i in range(RING):
                sp.wait_ge(pen_stored[i], 16 * HALF * NB)

            def load_scores(h, n, ready):
                sp.dma_start(ebc[:, h:h + n, :], e_dram[h:h + n, :].partition_broadcast(P)).then_inc(ready, 16)

            load_scores(0, 1, ebc_loaded[0])
            for k in range(2):
                sp.dma_start(a2[:, k, :], A[k * P:(k + 1) * P, :]).then_inc(a2_loaded[k], 16)
                load_scores(k + 1, 1, ebc_loaded[k + 1])
            sp.wait_ge(G[0]["gru_done"], NB * KC)
            load_scores(HEADS, HEADS, ebc_loaded[HEADS])
            sp.dma_start(w0, W0.rearrange("(c p) n -> p c n", p=P)).then_inc(w0_loaded, 16)
            for dst, src in ((gw[:, 0, :, :], nWi.rearrange("(c p) n -> p c n", p=P)),
                             (gw[:, 1, :, :], nWh.rearrange("(c p) n -> p c n", p=P)), (bi, nbi), (bh, nbh)):
                sp.dma_start(dst, src).then_inc(ngw_loaded, 16)
            with sp.Fori(0, JT // 2 - 1) as t:
                for k in range(2):
                    sp.wait_ge(rowmax_done, 2 * t + (k + 1))
                    sp.dma_start(a2[:, k, :], A[ds((2 * t + (2 + k)) * P, P), :]).then_inc(a2_loaded[k], 16)

            sp.wait_ge(rowmax_done, JT)
            for i, (t0, t1) in enumerate(CHUNKS):
                sp.dma_start(xt2[:, :, t0 * P:t1 * P], xT.rearrange("(c p) n -> p c n", p=P)[:, :, t0 * P:t1 * P]
                             ).then_inc(xt2_loaded[i], 16)
            sp.wait_ge(exp_done, HEADS * JT)
            for j in range(RING):
                load_tile(0, j)
            sp.wait_ge(nmT_ready, 2)
            for i, rows in enumerate((nmT, rdT)):
                sp.dma_start(nm_dram[HEADS * i:HEADS * (i + 1), :].rearrange("h (t p) -> (h t) p", p=P),
                             rows[0:HEADS * JT, :]).then_inc(nm_stored, 16)
            sp.wait_ge(nm_stored, 32)
            sp.wait_ge(hw_mm, 2 * JT)

            def load_maxima(b):
                if not isinstance(b, int) or b > 0:
                    sp.wait_ge(arg_ready, b * JT)
                sp.dma_start(negm, nm_dram[0:HEADS, ds(b * IB, IB)].partition_broadcast(P)).then_inc(negm_loaded, 16)

            stream(u_ready, NB, IB, load_maxima)

            sp.wait_ge(G[1]["gate_mm"], NB * KC * 4)
            sp.dma_start(wall[:, :, 0:H], W1.rearrange("(c p) n -> p c n", p=P)).then_inc(wall_loaded, 16)
            sp.wait_ge(strow_ready, JT)
            sp.dma_start(s_dram[:, 0:NP], strow[0:H1, :]).then_inc(s_stored, 16)
            sp.dma_start(s_dram[:, NP:NP + IB1], strow[0:H1, 0:IB1]).then_inc(s_stored, 16)
            sp.wait_ge(tmax_ready, 1)
            sp.dma_start(t_dram.rearrange("a h -> h a"), tmax[0:2 * H1, :]).then_inc(s_stored, 16)
            sp.wait_ge(s_stored, 48)
            sp.dma_start(tb, t_dram.partition_broadcast(P).rearrange("p a n -> p (a n)")).then_inc(tb_loaded, 16)

            sp.wait_ge(parts_ready, JT)
            for j in range(RING):
                load_tile(0, j, IB1)
            stream(mask_ready, NB1, IB1, lambda b: None)
            sp.wait_ge(o_stored, 16 * NB1)

        def pe_gates(pe, S, p, c, names, inT, hT):
            q = p * KC + c
            for name in names:
                m, sources, dst, before = {
                    "r": (c, (0, 1), bank[6], ("hn_read", q)), "z": (KC + c, (0, 1), bank[7], ("pre_ready", q)),
                    "hn": (2 * KC + c, (1,), bank[6], ("r_read", q + 1)),
                    "in": (2 * KC + c, (0,), bank[7], ("z_read", q + 1))}[name]
                if c > 0 or name in ("hn", "in"):
                    pe.wait_ge(S[before[0]], before[1])
                terms = [(s, kc) for s in sources for kc in range(KC)]
                for n, (s, kc) in enumerate(terms):
                    mm = pe.matmul(dst[:, 0:IB], gw[:, s, kc, m * P:(m + 1) * P], (inT, hT)[s](kc),
                                   start=(n == 0), stop=(n == len(terms) - 1))
                mm.then_inc(S["gate_mm"], 1)

        def act_rz(act, S, p, c, buf):
            q = p * KC + c
            if c > 0:
                act.wait_ge(S["out_ready"], q)
            act.wait_ge(S["gate_mm"], 4 * q + 1)
            act.activation(buf[0], bank[6][:, 0:IB], ACT.Tanh, bias=brz[:, c:c + 1], scale=0.5).then_inc(S["r_read"], 1)
            act.wait_ge(S["gate_mm"], 4 * q + 2)
            act.activation(buf[1], bank[7][:, 0:IB], ACT.Tanh, bias=brz[:, KC + c:KC + c + 1],
                           scale=0.5).then_inc(S["z_read"], 1)

        def act_hn(act, S, p, c, buf):
            act.wait_ge(S["gate_mm"], 4 * (p * KC + c) + 3)
            act.activation(buf[2], bank[6][:, 0:IB], ACT.Identity, bias=bh[:, 4 + c:5 + c]).then_inc(S["hn_read"], 1)

        def act_n(act, S, p, c, buf):
            act.wait_ge(S["pre_ready"], p * KC + c + 1)
            act.activation(buf[3], buf[2], ACT.Tanh, bias=bi[:, 4 + c:5 + c]).then_inc(S["n_ready"], 1)

        GRU_LINKS = 4

        def vec_pre(dve, S, p, c, buf, sem):
            tr, hq = buf[0], buf[2]
            q = p * KC + c
            cnt = Count(dve, sem)
            cnt.at(q * GRU_LINKS)
            dve.wait_ge(S["hn_read"], q + 1)
            cnt.link(dve.scalar_tensor_tensor(hq, tr, 1.0, hq, ALU.add, ALU.mult))
            dve.wait_ge(S["gate_mm"], 4 * q + 4)
            dve.scalar_tensor_tensor(hq, hq, 0.5, bank[7][:, 0:IB], ALU.mult, ALU.add).then_inc(S["pre_ready"], 1)

        def vec_out(dve, S, p, c, buf, xin, dg, sem):
            tz, nn, dx = buf[1], buf[3], buf[4 + c]
            q = p * KC + c
            cnt = Count(dve, sem)
            cnt.at(q * GRU_LINKS + 1)
            dve.wait_ge(S["n_ready"], q + 1)
            cnt.link(dve.tensor_tensor(dx, xin(c), nn, ALU.subtract))
            cnt.link(dve.scalar_tensor_tensor(dx, tz, 1.0, dx, ALU.add, ALU.mult))
            dve.scalar_tensor_tensor(dx, dx, 0.5, nn, ALU.mult, ALU.add).then_inc(S["out_ready"], 1)
            dve.wait_ge(S["out_ready"], q + 1)
            cnt.link(dve.tensor_tensor(dx, dx, dg, ALU.mult))

        def vec_add(dve, S, p, buf):
            dve.wait_ge(S["gate_mm"], p * (4 * KC) + 4 * KC)
            for c in range(KC):
                y = yT[:, c, ds(p * IB, IB)]
                dve.tensor_tensor(y, y, buf[4 + c], ALU.add).then_inc(S["gru_done"], 1)

        @block.tensor
        def _(pe):
            pe.wait_ge(setup_loaded, 16 * 7)
            for h in range(HEADS):
                for kc in range(KC):
                    for oc in range(KC):
                        pe.matmul(bank[0][:, kc * NV + 2 * h:kc * NV + 2 * h + 2],
                                  w0t[:, h * KC + oc, kc * P:(kc + 1) * P], a0_sb[:, oc, h, :],
                                  start=(oc == 0), stop=(oc == KC - 1))
            for h in range(H1):
                for kc in range(KC):
                    o = kc * 2 * H1 + 2 * h
                    mm = pe.matmul(bank[1][:, o:o + 2], w1t[0:FO, h, kc * P:(kc + 1) * P], a1_sb[0:FO, h, :],
                                   start=True, stop=True)
            mm.then_inc(wa_done, 1)
            pe.wait_ge(wa_ready, 1)
            pe.wait_ge(xT_loaded, 16)
            for t in range(JT):
                for kc in range(KC):
                    mm = pe.matmul(bank[2][:, t * NV:(t + 1) * NV], yT[:, kc, t * P:(t + 1) * P], wa[:, kc, :],
                                   start=(kc == 0), stop=(kc == KC - 1))
            mm.then_inc(u_done, 1)

            pe.wait_ge(upar_ready, 1)
            def edge_piece(p, n):
                if n == 0:
                    pe.wait_ge(support_evac, 4 * p + 4)
                    pe.matmul(bank[4][0:CNT + 1, 0:IB], sel_sb[0:19, 0, :], usum[0:19, 0, :], start=True, stop=False)
                    pe.matmul(bank[4][0:CNT + 1, 0:IB], sel_sb[0:19, 1, :], usum[0:19, 1, :], start=False,
                              stop=True).then_inc(sel_done, 1)
                else:
                    if n == 1:
                        pe.wait_ge(egw_loaded, 32)
                    c, names = divmod(n - 1, 2)
                    pe_gates(pe, G[0], p, c, (("r", "z"), ("hn", "in"))[names], lambda kc: nsT[:, kc, :],
                             lambda kc: yT[:, kc, ds(p * IB, IB)])

            def support(b, p):
                for j in range(JT):
                    pe.wait_ge(support_in, b * JT + (j + 1))
                    def bank_read(i):
                        if j == 0 and p is not None:
                            pe.wait_ge(support_evac, p * 4 + (i + 1))

                    if p is None and j in [t0 for t0, _ in CHUNKS]:
                        pe.wait_ge(x_loaded[[t0 for t0, _ in CHUNKS].index(j)], 16)
                    first, last = j == 0, j == JT - 1
                    for c in range(KC):
                        bank_read(c)
                        pe.matmul(bank[c][:, 0:IB], x_sb[:, j, c * P:(c + 1) * P], am[:, j % RING, :], start=first, stop=last)
                    bank_read(2)
                    pe.matmul(bank[2][0:19, 0:IB], upar[:, j, 0:19], pos[:, j % RING, :], start=first, stop=last)
                    bank_read(3)
                    pe.matmul(bank[3][0:19, 0:IB], upar[:, j, 0:19], neg[:, j % RING, :], start=first,
                              stop=last).then_inc(support_mm, 1)
                    if p is not None and j in (1, 3, 6, 10, 13):
                        edge_piece(p, (1, 3, 6, 10, 13).index(j))
                pe.wait_ge(zs_ready, b) if p is not None else None

            support(0, None)
            with pe.Fori(1, NB) as b:
                support(b, b - 1)
            edge_piece(NB - 1, 0)
            pe.wait_ge(e_ready, NB)
            for t in range(JT):
                mm = pe.transpose(bank[5][:, t * NV:(t + 1) * NV], escore[0:NV, t * P:(t + 1) * P], ident[0:NV, 0:NV])
            mm.then_inc(ecol_mm, 1)
            for n in range(1, 5):
                edge_piece(NB - 1, n)
            pe.wait_ge(nm_ready, 2)
            pe.transpose(bank[4][0:HEADS * JT, 0:P], nm, ident[:, :])
            pe.transpose(bank[4][0:HEADS * JT, P:2 * P], rd, ident[:, :]).then_inc(nm_mm, 1)

            pe.wait_ge(w0_loaded, 16)
            pe.wait_ge(ecol_ready, 1)
            pe.wait_ge(nmT_ready, 2)
            half = HEADS * H // 2
            for t in range(JT):
                if t in [t0 for t0, _ in CHUNKS]:
                    pe.wait_ge(xt2_loaded[[t0 for t0, _ in CHUNKS].index(t)], 16)
                for n in range(2):
                    if t >= 4:
                        pe.wait_ge((hw_evac_a, hw_evac_v)[n], t - 3)
                    for kc in range(KC):
                        mm = pe.matmul(bank[(2 * t + n) % 8][:, 0:half], xt2[:, kc, t * P:(t + 1) * P],
                                       w0[:, kc, n * half:(n + 1) * half], start=(kc == 0), stop=(kc == KC - 1))
                    mm.then_inc(hw_mm, 1)

            pe.wait_ge(hw_evac_a, JT)
            pe.wait_ge(hw_evac_v, JT)
            pe.wait_ge(ngw_loaded, 64)
            def node_piece(p, n):
                c, names = divmod(n, 2)
                pe_gates(pe, G[1], p, c, (("r", "z"), ("hn", "in"))[names], lambda kc: esT[:, kc, :],
                         lambda kc: xTb[:, kc, :])

            def attend(b, p):
                for j in range(JT):
                    pe.wait_ge(u_ready, b * JT + (j + 1))
                    for h in range(HEADS):
                        for c in range(KC):
                            if j == 0 and p is not None:
                                pe.wait_ge(num_evac, p * (HEADS * KC) + (KC * h + c + 1))
                            mm = pe.matmul(bank[KC * h + c][:, 0:IB], hw[:, j, h * H + c * P:h * H + (c + 1) * P],
                                           u[:, j % 2, h, :], start=(j == 0), stop=(j == JT - 1))
                    mm.then_inc(attend_mm, 1)
                    if p is not None and j == 6:
                        pe.wait_ge(xTb_loaded, p * 32 + 32)
                    if p is not None and j in (6, 8, 11, 14):
                        pe.wait_ge(es_ready, p + 1)
                        node_piece(p, (6, 8, 11, 14).index(j))
                if p is not None:
                    pe.wait_ge(G[1]["hn_read"], p * KC + KC)
                    pe.wait_ge(G[1]["pre_ready"], p * KC + KC)

            attend(0, None)
            with pe.Fori(1, NB) as b:
                attend(b, b - 1)
            pe.wait_ge(es_ready, NB)
            pe.wait_ge(xTb_loaded, 32 * NB)
            for n in range(4):
                node_piece(NB - 1, n)

            pe.wait_ge(wall_loaded, 16)
            pe.wait_ge(bias_ready, 3)
            def norm_front(tt):
                if not isinstance(tt, int):
                    pe.wait_ge(xs_ready, 2 * tt)
                for k in range(2):
                    pe.wait_ge(ys_ready, 2 * tt + (k + 1))
                    for c in range(KC):
                        mm = pe.transpose(bank[k][:, c * P:(c + 1) * P], ys[:, k, c, :], ident[:, :])
                    mm.then_inc(yt_mm, 1)

            def norm_back(tt):
                for k in range(2):
                    pe.wait_ge(xs_ready, 2 * tt + (k + 1))
                    for c in range(KC):
                        mm = pe.transpose(bank[2 + k][:, c * P:(c + 1) * P], xs[:, k, c * P:(c + 1) * P], ident[:, :])
                    mm.then_inc(x1T_mm, 1)

            def project(tt):
                for k in range(2):
                    pe.wait_ge(x1T_ready, 2 * tt + (k + 1))
                    for c in range(KC):
                        pe.matmul(bank[4 + k][:, 0:H + 2 * H1], x1T[:, k, c, :], wall[:, c, :], start=(c == 0), stop=(c == KC - 1))
                    for c in range(KC):
                        mm = pe.matmul(bank[6 + k][0:2 * H1, 0:P], wa1[:, c, :], x1T[:, k, c, :], start=(c == 0), stop=(c == KC - 1))
                    mm.then_inc(wh_mm, 1)

            norm_front(0)
            with pe.Fori(1, JT // 2) as tt:
                norm_back(tt - 1)
                norm_front(tt)
                project(tt - 1)
                pe.wait_ge(strow_ready, 2 * tt)
                pe.wait_ge(wh_ready, 2 * tt)
            norm_back(JT // 2 - 1)
            project(JT // 2 - 1)

            def gat(b):
                first_block = isinstance(b, int)
                for j in range(JT):
                    pe.wait_ge(g_ready, b * JT + (j + 1))
                    for c in range(IT1):
                        for h in range(H1):
                            n = c * H1 + h
                            if j == 0 and not first_block:
                                pe.wait_ge(ev_ready, b * (IT1 * H1) + (n + 1 - IT1 * H1))
                            for q in range(2):
                                mm = pe.matmul(bank[n][:, q * PW:(q + 1) * PW], g[:, j % 2, q, h, c * P:(c + 1) * P],
                                               parts[:, j, h, q, :, :].rearrange("p a b -> p (a b)"),
                                               start=(j == 0 and q == 0), stop=(j == JT - 1), skip_group_check=True)
                    mm.then_inc(gat_mm, 1)

            pe.wait_ge(parts_ready, JT)
            gat(0)
            with pe.Fori(1, NB1) as b:
                gat(b)

        @block.gpsimd
        def _(pool):
            pool.memset(offdiag[:, :], 1.0).then_inc(pool_chain, 1)
            pool.memset(ident[:, :], 0.0).then_inc(pool_chain, 1)
            pool.memset(zdiag[:, :], 0.0).then_inc(pool_chain, 1)
            pool.memset(eps, EPS).then_inc(const_ready, 1)
            pool.wait_ge(pool_chain, 3)
            for v, fill in ((ident, 1.0), (zdiag, -BIG)):
                pool.affine_select(out=v[:, :], in_=v[:, :], compare_op=ALU.not_equal, fill=fill, base=0,
                                   pattern=[[-1, P]], channel_multiplier=1).then_inc(const_ready, 1)
            mid = offdiag[:, NP:NP + P]
            pool.affine_select(out=mid, in_=mid, compare_op=ALU.not_equal, fill=0.0, base=0,
                               pattern=[[-1, P]], channel_multiplier=1).then_inc(const_ready, 1)

        @block.scalar
        def _(act):
            act.wait_ge(bias_ready, 1)

            def load_diag(b):
                act.dma_start(diag1, diag[:, ds(b * IB, IB)].partition_broadcast(P).rearrange("p a n -> p (a n)")
                              ).then_inc(diag_loaded, 16)

            def edge_piece(p, n):
                if n == 0:
                    act.wait_ge(sel_done, p + 1)
                    act.copy(zs[0:CNT + 1, :], bank[4][0:CNT + 1, 0:IB]).then_inc(zs_ready, 1)
                else:
                    c, piece = divmod(n - 1, 3)
                    (act_rz, act_hn, act_n)[piece](act, G[0], p, c, gru1)

            EDGE_STEPS = (7, 9, 12, 14, 16, 19, 21)

            def support(b, p):
                for j in range(JT):
                    act.wait_ge(support_in, b * JT + (j + 1))
                    act.dma_start(pen_dram[P * j:P * (j + 1), ds(b * IB, IB)], penw[:, j % RING, :]
                                  ).then_inc(pen_stored[j % RING], 16)
                    if p is not None and j in EDGE_STEPS:
                        edge_piece(p, EDGE_STEPS.index(j))
                if p is not None:
                    act.wait_ge(e_ready, p + 1)
                    act.wait_ge(G[0]["gru_done"], p * KC + KC)
                    load_diag(b)

            load_diag(0)
            support(0, None)
            with act.Fori(1, NB) as b:
                support(b, b - 1)
            for n in range(7):
                edge_piece(NB - 1, n)

            def exps(t, k, n):
                for h in range(HEADS):
                    slot = (HEADS * k + h) % 2
                    act.wait_ge(max_ready, n + (h + 1))
                    act.activation(args[slot], args[slot], ACT.Exp, bias=mneg[:, k, h:h + 1],
                                   accum_out=dsum[:, k, h:h + 1]).then_inc(exp_done, 1)
                act.wait_ge(exp_done, n + HEADS)
                act.copy(dcol[:, ds(t, 1), :].rearrange("p a h -> p (a h)"), dsum[:, k, :]).then_inc(den_ready, 1)

            with act.Fori(0, JT // 2) as tt:
                for k in range(2):
                    exps(2 * tt + k, k, (2 * HEADS) * tt + HEADS * k)

            half = HEADS * H // 2
            act.wait_ge(rowmax_done, JT)
            for t in range(JT):
                act.wait_ge(hw_mm, 2 * t + 1)
                act.copy(hw[:, t, 0:half], bank[(2 * t) % 8][:, 0:half]).then_inc(hw_evac_a, 1)

            act.wait_ge(bias_ready, 2)
            for i in range(RING):
                act.wait_ge(pen_stored[i], 16 * HALF * NB)

            def load_pen(b, j):
                act.dma_start(penr[:, j % 2, :], pen_dram[P * j:P * (j + 1), ds(b * IB, IB)]
                              ).then_inc(pen_loaded[j % 2], 16)

            def load_xT(b):
                act.dma_start(diag3, diag[:, ds(b * IB, IB)].partition_broadcast(P).rearrange("p a n -> p (a n)")
                              ).then_inc(xTb_loaded, 16)
                act.dma_start(xTb, xT.rearrange("(c p) n -> p c n", p=P)[:, :, ds(b * IB, IB)]).then_inc(xTb_loaded, 16)

            def load_rd(b):
                act.dma_start(rdr, nm_dram[HEADS:2 * HEADS, ds(b * IB, IB)].partition_broadcast(P)).then_inc(rd_loaded, 16)

            def evacuate(p):
                act.wait_ge(attend_mm, p * JT + JT)
                for i in range(HEADS * KC):
                    act.copy(nums[i], bank[i][:, 0:IB]).then_inc(num_evac, 1)

            ACT_STEPS = (7, 9, 11, 13, 15, 17)

            def attend(b, p):
                for j in range(2):
                    load_pen(b, j)
                for j in range(JT):
                    act.wait_ge(arg_ready, b * JT + (j + 1))
                    for h in range(HEADS):
                        act.activation(wgt[:, j % 2, h, :], wgt[:, j % 2, h, :], ACT.Exp,
                                       bias=ebias[:, j, h:h + 1]).then_inc(wgt_ready, 1)
                    if j + 2 < JT:
                        load_pen(b, j + 2)
                    if p is None:
                        continue
                    if j == 0:
                        evacuate(p)
                    if j == 4:
                        act.wait_ge(es_ready, p + 1)
                        load_rd(b)
                    if j in ACT_STEPS:
                        c, n = divmod(ACT_STEPS.index(j), 3)
                        (act_rz, act_hn, act_n)[n](act, G[1], p, c, gru3)
                if p is not None:
                    act.wait_ge(G[1]["gru_done"], p * KC + KC)
                    load_xT(b)

            act.wait_ge(nm_stored, 32)
            act.wait_ge(ebias_ready, 1)
            load_xT(0)
            load_rd(0)
            attend(0, None)
            with act.Fori(1, NB) as b:
                attend(b, b - 1)
            evacuate(NB - 1)
            for c in range(KC):
                for piece in (act_rz, act_hn, act_n):
                    piece(act, G[1], NB - 1, c, gru3)

            act.wait_ge(G[1]["gru_done"], NB * KC)
            act.wait_ge(const_ready, 4)
            def load_rows(tt):
                if not isinstance(tt, int):
                    act.wait_ge(yt_mm, 2 * tt)
                for k in range(2):
                    act.copy(ys[:, k, :, :], yT[:, :, ds((2 * tt + k) * P, P)]).then_inc(ys_ready, 1)

            def deviation(tt):
                act.wait_ge(var_ready, 2 * tt + 2)
                act.activation(sd, mv[:, :, 1], ACT.Sqrt, bias=eps).then_inc(sd_ready, 1)

            def x1_out(tt):
                for k in range(2):
                    act.wait_ge(x1T_mm, 2 * tt + (k + 1))
                    act.copy(x1T[:, k, :, :].rearrange("p c n -> p (c n)"), bank[2 + k][:, 0:H]).then_inc(x1T_ready, 1)
                for k in range(2):
                    act.activation(x1[:, 2 * tt + k, :], xs[:, k, :], ACT.Identity).then_inc(x1_stored, 1)

            def wh_out(tt):
                for k in range(2):
                    t = 2 * tt + k
                    act.wait_ge(wh_mm, t + 1)
                    act.copy(wh[:, t, :], bank[4 + k][:, 0:H])
                    act.copy(st[:, t, :], bank[4 + k][:, H:H + 2 * H1]).then_inc(wh_ready, 1)

            load_rows(0)
            deviation(0)
            with act.Fori(1, JT // 2) as tt:
                load_rows(tt)
                x1_out(tt - 1)
                deviation(tt)
                wh_out(tt - 1)
            x1_out(JT // 2 - 1)
            wh_out(JT // 2 - 1)

            act.wait_ge(ush_ready, 3)
            act.activation(bcoef[:, :, :, 0], ush, ACT.Exp).then_inc(coef_ready, 1)
            act.activation(bcoef[:, :, :, 1], ush, ACT.Exp, scale=SLOPE).then_inc(coef_ready, 1)
            act.activation(acoef[:, 0, :, :], acoef[:, 0, :, :], ACT.Exp, scale=1 - SLOPE).then_inc(coef_ready, 1)
            act.activation(acoef[:, 1, :, :], acoef[:, 1, :, :], ACT.Exp, scale=SLOPE - 1).then_inc(coef_ready, 1)

            act.wait_ge(s_stored, 48)
            def make_parts(t0, count):
                for i, ready in enumerate((fx_ready, hi_ready, mid_ready)):
                    for k in range(count):
                        act.wait_ge(ready, (t0 + (k + 1)) * 2 if i == 0 else t0 + (k + 1))
                        act.copy(parts[:, t0 + k, :, :, i, :].rearrange("p h q o -> p (h q) o"),
                                 fx[:, k].rearrange("p h q o -> p (h q) o")).then_inc((hi_cast, mid_cast, parts_ready)[i], 1)

            with act.Fori(0, JT // TILES) as r:
                make_parts(TILES * r, TILES)
            make_parts(JT // TILES * TILES, JT % TILES)
            act.wait_ge(parts_ready, JT)

            def load_scores(b, slot):
                act.dma_start(sbc[slot], s_dram[:, ds(b * IB1, IB1)].partition_broadcast(P)).then_inc(sbc_loaded[slot], 16)

            def gat(b, p, slot, loads):
                act.wait_ge(sbc_loaded[slot], loads * 16)
                for j in range(JT):
                    if j >= STEPS or p is not None:
                        act.wait_ge(pos_ready, b * JT + (j - STEPS + 1))
                    for h in range(H1):
                        ins = act.activation(sg[:, sg_slot(slot, j), h, :], sbc[slot][:, h, :], ACT.Sigmoid,
                                             bias=tsteep[:, j, h:h + 1], scale=STEEP)
                    ins.then_inc(sg_ready, 1)
                    if p is None:
                        if j == 2:
                            load_scores(1, 1)
                        continue
                    if j == 1:
                        gat_evac(p)
                    if j == 4:
                        act.wait_ge(sg_ready, b * JT)
                        load_scores(b + 1, 1 - slot)
                    if j == 17:
                        gat_sqrt(p)
                    if j == 21:
                        gat_store(p)

            def gat_evac(p):
                act.wait_ge(gat_mm, p * JT + JT)
                for c in range(IT1):
                    for h in range(H1):
                        act.copy(ev[:, c, h, :], bank[c * H1 + h][:, 0:2 * PW]).then_inc(ev_ready, 1)

            def gat_sqrt(p):
                act.wait_ge(var5, p * IT1 + IT1)
                act.activation(sd5, mv5[:, :, 1], ACT.Sqrt, bias=eps).then_inc(sd5_ready, 1)

            def gat_store(p):
                act.wait_ge(o_ready, p * IT1 + IT1)
                act.dma_start(out[ds(p * IB1, IB1), :].rearrange("(c p) f -> p c f", p=P), o5).then_inc(o_stored, 16)

            load_scores(0, 0)
            gat(0, None, 0, 1)
            with act.Fori(0, (NB1 - 1) // 2) as i:
                gat(2 * i + 1, 2 * i, 1, i + 1)
                gat(2 * i + 2, 2 * i + 1, 0, i + 2)
            for last in (gat_evac, gat_sqrt, gat_store):
                last(NB1 - 1)

        @block.vector
        def _(dve):
            chain = Count(dve, vec_chain)
            dve.wait_ge(wa_done, 1)
            chain.link(dve.tensor_copy(wa1[:, :, :].rearrange("p c (s h) -> p c s h", s=2),
                                       bank[1][:, 0:4 * H1].rearrange("p (c h s) -> p c s h", c=KC, s=2)))
            dve.tensor_copy(wa, bank[0][:, 0:KC * NV].rearrange("p (c v) -> p c v", c=KC)).then_inc(wa_ready, 1)
            dve.wait_ge(setup_loaded, 16 * 7)
            chain.link(dve.memset(mbig, -BIG))
            chain.link(dve.tensor_tensor(brz, bi[:, 0:4], bh[:, 0:4], ALU.add))
            dve.tensor_scalar(brz, brz, 0.5, None, ALU.mult).then_inc(bias_ready, 1)
            dve.wait_ge(u_done, 1)
            chain.link(dve.tensor_copy(u_sb, bank[2][:, 0:JT * NV].rearrange("p (t v) -> p t v", v=NV)))
            chain.link(dve.memset(upar[:, :, 18:20], 1.0))
            chain.link(dve.tensor_copy(upar[:, :, 0:NV], u_sb))
            chain.link(dve.tensor_tensor(u_r, u_sb, upar[:, :, 0:NV], ALU.subtract))
            chain.link(dve.tensor_copy(upar[:, :, NV:2 * NV], u_r))
            chain.link(dve.tensor_tensor(u_r, u_r, upar[:, :, NV:2 * NV], ALU.subtract))
            dve.tensor_copy(upar[:, :, 2 * NV:3 * NV], u_r).then_inc(upar_ready, 1)

            dve.wait_ge(const_ready, 4)
            dve.wait_ge(xT_loaded, 16)
            loop = Count(dve, support_chain)
            def evacuate_sums(p):
                dve.wait_ge(support_mm, p * JT + JT)
                for c in range(KC):
                    dve.tensor_copy(nsT[:, c, :], bank[c][:, 0:IB]).then_inc(support_evac, 1)
                for k in range(2):
                    dve.tensor_copy(usum[0:19, k, :], bank[2 + k][0:19, 0:IB]).then_inc(support_evac, 1)

            def edge_piece(p, n):
                if n == 0:
                    dve.wait_ge(zs_ready, p + 1)
                    dve.scalar_tensor_tensor(escore[0:CNT + 1, ds(p * IB, IB)], zs[0:CNT + 1, :], SLOPE,
                                             zs[0:CNT + 1, :], ALU.mult, ALU.max).then_inc(e_ready, 1)
                elif n in (1, 3):
                    vec_pre(dve, G[0], p, n // 2, gru1, gru_chain[0])
                elif n in (2, 4):
                    dve.wait_ge(diag_loaded, p * 16 + 16)
                    vec_out(dve, G[0], p, n // 2 - 1, gru1, lambda c: yT[:, c, ds(p * IB, IB)], diag1, gru_chain[0])
                else:
                    vec_add(dve, G[0], p, gru1)

            EVACUATE_STEP, EDGE_STEPS = 5, (8, 13, 15, 20, 22, 23)

            def support(b, p):
                for j in range(JT):
                    dve.wait_ge(tile_loaded[j % RING], 16 * (HALF * b + (j // RING + 1)))
                    if j >= RING or p is not None:
                        dve.wait_ge(support_mm, b * JT + (j - RING + 1))
                    if j >= RING or p is not None:
                        dve.wait_ge(pen_stored[j % RING], 16 * (HALF * b + j // RING))
                    loop.at(2 * (b * JT + j))
                    loop.link(dve.tensor_tensor(am[:, j % RING, :], ring[:, j % RING, :], window(j, b * IB, IB), ALU.mult))
                    loop.link(dve.tensor_scalar(pos[:, j % RING, :], am[:, j % RING, :], 0.0, None, ALU.is_gt))
                    dve.tensor_scalar(neg[:, j % RING, :], am[:, j % RING, :], 0.0, None, ALU.is_lt)
                    dve.tensor_scalar(penw[:, j % RING, :], pos[:, j % RING, :], -1.0, BIG, ALU.add,
                                      ALU.mult).then_inc(support_in, 1)
                    if p is not None and j == EVACUATE_STEP:
                        evacuate_sums(p)
                    if p is not None and j in EDGE_STEPS:
                        edge_piece(p, EDGE_STEPS.index(j))

            support(0, None)
            with dve.Fori(1, NB) as b:
                support(b, b - 1)
            evacuate_sums(NB - 1)
            edge_piece(NB - 1, 0)

            dve.wait_ge(e_ready, NB)
            chain.link(dve.tensor_reduce(flag[CNT:CNT + 1, :], escore[CNT:CNT + 1, :], AX.X, ALU.max))
            dve.tensor_copy(flag_i[CNT:CNT + 1, :], flag[CNT:CNT + 1, :]).then_inc(flag_ready, 1)
            dve.wait_ge(ecol_mm, 1)
            dve.tensor_copy(ecol, bank[5][:, 0:JT * NV].rearrange("p (t v) -> p t v", v=NV)).then_inc(ecol_ready, 1)
            for n in range(1, 6):
                edge_piece(NB - 1, n)
            dve.wait_ge(flag_ready, 1)
            negatives = dve.value_load(flag_i[CNT:CNT + 1, 0:1], min_val=0, max_val=NP)

            def rowmax(signed):
                loop = Count(dve, rowmax_chain[signed])
                LINKS = 2 + HEADS + signed * (2 + 3 * HEADS)

                def tile(t, k, tt, first):
                    n0 = (2 * HEADS) * tt + HEADS * k
                    loop.at(t * LINKS)
                    if signed and first and k == 0:
                        dve.wait_ge(ebc_loaded[HEADS], 16)
                    dve.wait_ge(a2_loaded[k], tt * 16 + 16)
                    loop.link(dve.tensor_scalar(pen2, a2[:, k, :], 0.0, -BIG, ALU.is_le, ALU.mult))
                    own = pen2[:, ds(t * P, P)]
                    loop.link(dve.tensor_tensor(own, own, zdiag[:, :], ALU.min))
                    if signed:
                        own = a2[:, k, ds(t * P, P)]
                        loop.link(dve.tensor_scalar(a2[:, k, :], a2[:, k, :], 0.0, -BIG, ALU.is_ge, ALU.mult))
                        loop.link(dve.tensor_tensor(own, own, zdiag[:, :], ALU.min))
                    for h in range(HEADS):
                        slot = (HEADS * k + h) % 2
                        n = HEADS * k + h
                        if first and k == 0:
                            dve.wait_ge(ebc_loaded[h], 16)
                        if not first or n >= 2 - signed:
                            dve.wait_ge(exp_done, n0 + (h + signed - 1))
                        if not signed:
                            dve.memset(cell, 0.0)
                            ins = dve.tensor_tensor_reduce(args[slot], ebc[:, h, :], pen2, 1.0, -3.0e38, ALU.add, ALU.max,
                                                           mrow[:, k, h:h + 1])
                        else:
                            other = args[1 - slot]
                            loop.link(dve.tensor_tensor(args[slot], ebc[:, h, :], pen2, ALU.add))
                            loop.link(dve.tensor_tensor(other, ebc[:, HEADS + h, :], a2[:, k, :], ALU.add))
                            loop.settle(dve.tensor_tensor(args[slot], args[slot], other, ALU.max), cell)
                            ins = dve.tensor_reduce(mrow[:, k, h:h + 1], args[slot], AX.X, ALU.max)
                        loop.link(ins)
                        dve.tensor_scalar(mneg[:, k, h:h + 1], mrow[:, k, h:h + 1], -1.0, BIG / 2, ALU.mult,
                                          ALU.min).then_inc(max_ready, 1)
                    assert loop.k == LINKS
                    dve.wait_ge(max_ready, n0 + HEADS)
                    dve.tensor_scalar(mcol[:, ds(t, 1), :].rearrange("p a h -> p (a h)"), mneg[:, k, :], 1.0, None,
                                      ALU.mult).then_inc(rowmax_done, 1)

                for k in range(2):
                    tile(k, k, 0, True)
                with dve.Fori(1, JT // 2) as tt:
                    for k in range(2):
                        tile(2 * tt + k, k, tt, False)

            with dve.If(negatives > 0):
                rowmax(True)
            with dve.Else():
                rowmax(False)
            dve.wait_ge(rowmax_done, JT)
            dve.tensor_scalar(nm.rearrange("p (h t) -> p t h", h=HEADS), mcol, 1.0, None, ALU.mult).then_inc(nm_ready, 1)
            dve.wait_ge(den_ready, JT)
            chain.link(dve.tensor_scalar(dcol, dcol, TINY, float(HEADS), ALU.max, ALU.mult))
            chain.link(dve.reciprocal(dcol, dcol))
            dve.tensor_scalar(rd.rearrange("p (h t) -> p t h", h=HEADS), dcol, 1.0, None, ALU.mult).then_inc(nm_ready, 1)
            dve.wait_ge(nm_mm, 1)
            dve.tensor_copy(nmT[0:HEADS * JT, :], bank[4][0:HEADS * JT, 0:P]).then_inc(nmT_ready, 1)
            dve.tensor_copy(rdT[0:HEADS * JT, :], bank[4][0:HEADS * JT, P:2 * P]).then_inc(nmT_ready, 1)

            half = HEADS * H // 2
            for t in range(JT):
                dve.wait_ge(hw_mm, 2 * t + 2)
                dve.tensor_copy(hw[:, t, half:2 * half], bank[(2 * t + 1) % 8][:, 0:half]).then_inc(hw_evac_v, 1)
            dve.wait_ge(ngw_loaded, 64)
            chain.link(dve.tensor_tensor(brz, bi[:, 0:4], bh[:, 0:4], ALU.add))
            dve.tensor_scalar(brz, brz, 0.5, None, ALU.mult).then_inc(bias_ready, 1)

            dve.wait_ge(nm_stored, 32)
            AVERAGE_LINKS = KC + (HEADS - 1) * 2 * KC - 1

            def attend_all(signed):
                loop = Count(dve, attend_chain[signed])
                STEP = 2 + 3 * HEADS - 1
                if signed:
                    dve.memset(ebias, 0.0).then_inc(ebias_ready, 1)
                else:
                    dve.tensor_scalar(ebias, ecol[:, :, 0:HEADS], 1.0, None, ALU.mult).then_inc(ebias_ready, 1)

                def arguments(b, p, j):
                    s = j % 2
                    tile = ring[:, j % RING, :]
                    dve.wait_ge(tile_loaded[j % RING], 16 * (HALF * NB + HALF * b + (j // RING + 1)))
                    dve.wait_ge(pen_loaded[s], 16 * (b * (JT // 2) + (j // 2 + 1)))
                    if j >= 2 or p is not None:
                        dve.wait_ge(u_ready, b * JT + (j - 1))
                    if not signed:
                        dve.tensor_tensor(wgt[:, s, :, :], negm, penr[:, s, :].unsqueeze(1).to_broadcast([P, HEADS, IB]),
                                          ALU.add).then_inc(arg_ready, 1)
                        return
                    loop.at((b * JT + j) * STEP)
                    for h in range(HEADS):
                        loop.link(dve.scalar_tensor_tensor(wgt[:, s, h, :], negm[:, h, :], ecol[:, j, h:h + 1],
                                                           penr[:, s, :], ALU.add, ALU.min))
                    loop.link(dve.scalar_tensor_tensor(mask3, tile, 0.0, window(j, b * IB, IB), ALU.is_lt, ALU.mult))
                    loop.link(dve.tensor_scalar(pen3, mask3, -1.0, BIG, ALU.add, ALU.mult))
                    for h in range(HEADS):
                        loop.link(dve.scalar_tensor_tensor(argn, negm[:, h, :], ecol[:, j, HEADS + h:HEADS + h + 1],
                                                           pen3, ALU.add, ALU.min))
                        ins = dve.tensor_tensor(wgt[:, s, h, :], wgt[:, s, h, :], argn, ALU.max)
                        if h < HEADS - 1:
                            loop.link(ins)
                    ins.then_inc(arg_ready, 1)
                    assert loop.k == STEP

                def products(b, p, j):
                    s = j % 2
                    dve.wait_ge(wgt_ready, (b * JT + (j + 1)) * HEADS)
                    if j >= 2 or p is not None:
                        dve.wait_ge(attend_mm, b * JT + (j - 1))
                    dve.tensor_tensor(u[:, s, :, :], wgt[:, s, :, :],
                                      ring[:, j % RING, :].unsqueeze(1).to_broadcast([P, HEADS, IB]),
                                      ALU.mult).then_inc(u_ready, 1)

                def node_piece(p, n):
                    if n in (0, 2):
                        vec_pre(dve, G[1], p, n // 2, gru3, gru_chain[1])
                    elif n in (1, 3):
                        dve.wait_ge(xTb_loaded, p * 32 + 32)
                        vec_out(dve, G[1], p, n // 2, gru3, lambda c: xTb[:, c, :], diag3, gru_chain[1])
                    else:
                        vec_add(dve, G[1], p, gru3)

                def average(p, h):
                    cnt = Count(dve, es_chain)
                    cnt.at(p * AVERAGE_LINKS + (0, KC, 3 * KC)[h])
                    dve.wait_ge(rd_loaded, p * 16 + 16)
                    for c in range(KC):
                        dve.wait_ge(num_evac, p * (HEADS * KC) + (KC * h + c + 1))
                        num3 = nums[KC * h + c]
                        if h == 0:
                            cnt.link(dve.tensor_tensor(esT[:, c, :], num3, rdr[:, h, :], ALU.mult))
                            continue
                        cnt.link(dve.tensor_tensor(term, num3, rdr[:, h, :], ALU.mult))
                        ins = dve.tensor_tensor(esT[:, c, :], esT[:, c, :], term, ALU.add)
                        if h == HEADS - 1 and c == KC - 1:
                            ins.then_inc(es_ready, 1)
                        else:
                            cnt.link(ins)

                VEC_STEPS = (10, 12, 16, 18, 20)

                def attend(b, p):
                    dve.wait_ge(negm_loaded, b * 16 + 16)
                    for j in range(JT + 1):
                        if j < JT:
                            arguments(b, p, j)
                        if j > 0:
                            products(b, p, j - 1)
                        if p is not None and j in (1, 2, 3):
                            average(p, j - 1)
                        if p is not None and j in VEC_STEPS:
                            node_piece(p, VEC_STEPS.index(j))

                attend(0, None)
                with dve.Fori(1, NB) as b:
                    attend(b, b - 1)
                for h in range(HEADS):
                    average(NB - 1, h)
                for n in range(5):
                    node_piece(NB - 1, n)

            with dve.If(negatives > 0):
                attend_all(True)
            with dve.Else():
                attend_all(False)

            dve.wait_ge(G[1]["gate_mm"], NB * KC * 4)
            dve.tensor_copy(wall[:, :, H:H + 2 * H1], wa1[:, :, :]).then_inc(bias_ready, 1)
            chain.link(dve.tensor_scalar(offdiag[:, :], offdiag[:, :], -1.0, 1.0, ALU.mult, ALU.add))
            def norm_front(tt):
                loop = Count(dve, norm_chain)
                loop.at(tt * 3)
                for k in range(2):
                    dve.wait_ge(yt_mm, 2 * tt + (k + 1))
                    loop.settle(dve.bn_stats(stats[:, k, :], bank[k][:, 0:H]), cell)
                    dve.bn_aggr(mv[:, k, :], stats[:, k, :]).then_inc(var_ready, 1)
                dve.wait_ge(sd_ready, tt + 1)
                loop.link(dve.reciprocal(rstd, sd))
                if not isinstance(tt, int):
                    dve.wait_ge(x1_stored, 2 * tt)
                for k in range(2):
                    dve.tensor_scalar(xs[:, k, :], bank[k][:, 0:H], mv[:, k, 0:1], rstd[:, k:k + 1], ALU.subtract,
                                      ALU.mult).then_inc(xs_ready, 1)

            def rows_out(tt):
                for k in range(2):
                    t = 2 * tt + k
                    dve.wait_ge(wh_mm, t + 1)
                    dve.tensor_copy(strow[0:2 * H1, ds(t * P, P)], bank[6 + k][0:2 * H1, 0:P]).then_inc(strow_ready, 1)

            norm_front(0)
            with dve.Fori(1, JT // 2) as tt:
                norm_front(tt)
                rows_out(tt - 1)
            rows_out(JT // 2 - 1)

            dve.wait_ge(strow_ready, JT)
            dve.tensor_reduce(tmax[0:2 * H1, :], strow[0:2 * H1, 0:N], AX.X, ALU.max).then_inc(tmax_ready, 1)
            dve.wait_ge(tb_loaded, 16)
            dve.wait_ge(wh_ready, JT)
            dve.wait_ge(ys_ready, JT)
            s_col, t_col = st[:, :, 0:H1], st[:, :, H1:2 * H1]
            t_top = tb[:, H1:2 * H1].unsqueeze(1).to_broadcast([P, JT, H1])
            chain.link(dve.tensor_tensor(ush, t_col, t_top, ALU.subtract))
            dve.tensor_scalar(ush, ush, 0.0, None, ALU.min).then_inc(ush_ready, 1)
            chain.link(dve.tensor_tensor(acoef[:, 1, :, :], s_col, t_top, ALU.add))
            chain.link(dve.tensor_scalar(acoef[:, 0, :, :], acoef[:, 1, :, :], 0.0, None, ALU.min))
            dve.tensor_scalar(acoef[:, 1, :, :], acoef[:, 1, :, :], 0.0, None, ALU.max).then_inc(ush_ready, 1)
            dve.tensor_scalar(tsteep, t_col, STEEP, None, ALU.mult).then_inc(ush_ready, 1)

            dve.wait_ge(coef_ready, 4)
            def make_parts(t0, count):
                for k in range(count):
                    t = t0 + k
                    dve.tensor_tensor(fx[:, k, :, :, 0:FO],
                                      wh[:, t, :].rearrange("p (h o) -> p h o", h=H1).unsqueeze(2).to_broadcast(
                                          [P, H1, 2, FO]),
                                      bcoef[:, t, :, :].unsqueeze(3).to_broadcast([P, H1, 2, FO]),
                                      ALU.mult).then_inc(fx_ready, 1)
                    dve.tensor_scalar(fx[:, k, :, :, FO:FP].rearrange("p h q o -> p h (q o)"),
                                      bcoef[:, ds(t, 1), :, :].rearrange("p a h q -> p (a h) q"), 1.0, None,
                                      ALU.mult).then_inc(fx_ready, 1)
                for cast, i, ready in ((hi_cast, 0, hi_ready), (mid_cast, 1, mid_ready)):
                    for k in range(count):
                        f = fx[:, k].rearrange("p h q o -> p (h q) o")
                        dve.wait_ge(cast, t0 + (k + 1))
                        part = parts[:, t0 + k, :, :, i, :].rearrange("p h q o -> p (h q) o")
                        dve.tensor_tensor(f, f, part, ALU.subtract).then_inc(ready, 1)
                dve.wait_ge(parts_ready, t0 + count)

            with dve.Fori(0, JT // TILES) as r:
                make_parts(TILES * r, TILES)
            make_parts(JT // TILES * TILES, JT % TILES)

            def gat_mask(b, j):
                first_block = isinstance(b, int)
                dve.wait_ge(tile_loaded[j % RING], 16 * (2 * HALF * NB + HALF * b + (j // RING + 1)))
                if j >= 2 or not first_block:
                    dve.wait_ge(g_ready, b * JT + (j - 1))
                dve.scalar_tensor_tensor(mask5[:, j % 2, :], ring[:, j % RING, 0:IB1], 0.0, window(j, b * IB1, IB1),
                                         ALU.not_equal, ALU.max).then_inc(mask_ready, 1)

            def gat(b, p, odd):
                first_block = isinstance(b, int)
                gat_mask(b, 0)
                for j in range(JT):
                    s = j % 2
                    m = mask5[:, s, :].unsqueeze(1).to_broadcast([P, H1, IB1])
                    dve.wait_ge(mask_ready, b * JT + (j + 1))
                    dve.wait_ge(sg_ready, b * JT + (j + 1))
                    if j >= 2 or not first_block:
                        dve.wait_ge(gat_mm, b * JT + (j - 1))
                    dve.tensor_tensor(g[:, s, 0, :, :], sg[:, sg_slot(odd, j), :, :], m, ALU.mult).then_inc(pos_ready, 1)
                    if j + 1 < JT:
                        gat_mask(b, j + 1)
                    dve.wait_ge(pos_ready, b * JT + (j + 1))
                    dve.tensor_tensor(g[:, s, 1, :, :], m, g[:, s, 0, :, :], ALU.subtract).then_inc(g_ready, 1)
                    if p is None:
                        continue
                    if 5 <= j < 5 + OUT_OPS:
                        gat_out(p, j - 5)
                    if j == 18:
                        gat_norm(p)
                if p is not None:
                    dve.wait_ge(o_stored, p * 16 + 16)

            OUT_OPS = 11

            def gat_out(p, n):
                if n == 0:
                    dve.wait_ge(ev_ready, (p + 1) * (IT1 * H1))
                else:
                    dve.wait_ge(out_chain, p * (OUT_OPS - 1) + n)
                e = ev.rearrange("p c h (q s o) -> p (c h q) s o", q=2, s=3)
                xq = xsum.rearrange("p h q o -> p (h q) o")
                y = y5.rearrange("p c (h o) -> p (c h) o", h=H1)

                def factor(q):
                    return acoef[:, q, ds(p * IT1, IT1), :].rearrange("p a h -> p (a h)").unsqueeze(2).to_broadcast(
                        [P, IT1 * H1, FP])

                if n == 0:
                    ins = dve.tensor_tensor(xq, e[:, :, 1, :], e[:, :, 2, :], ALU.add)
                elif n == 1:
                    ins = dve.tensor_tensor(xq, xq, e[:, :, 0, :], ALU.add)
                elif n == 2:
                    ins = dve.tensor_tensor(tmp5, xsum[:, :, 0, :], factor(0), ALU.mult)
                elif n == 3:
                    ins = dve.tensor_tensor(num, xsum[:, :, 1, :], factor(1), ALU.mult)
                elif n == 4:
                    ins = dve.tensor_tensor(num, num, tmp5, ALU.add)
                elif n == 5:
                    ins = dve.reciprocal(rd1, num[:, :, FO:FP].rearrange("p h o -> p (h o)"))
                elif n == 6:
                    ins = dve.tensor_tensor(y, num[:, :, 0:FO], rd1.unsqueeze(2).to_broadcast([P, IT1 * H1, FO]), ALU.mult)
                elif n == 7:
                    ins = dve.tensor_tensor(y5, y5, x1[:, ds(p * IT1, IT1), :], ALU.add)
                elif n in (8, 9):
                    ins = dve.bn_stats(stat5[:, n - 8, :], y5[:, n - 8, :])
                else:
                    dve.memset(cell, 0.0)
                    for c in range(IT1):
                        dve.bn_aggr(mv5[:, c, :], stat5[:, c, :]).then_inc(var5, 1)
                    return
                ins.then_inc(out_chain, 1)

            def gat_norm(p):
                cnt = Count(dve, gat_chain)
                cnt.at(p)
                dve.wait_ge(sd5_ready, p + 1)
                cnt.link(dve.reciprocal(rs5, sd5))
                for c in range(IT1):
                    dve.tensor_scalar(o5[:, c, :], y5[:, c, :], mv5[:, c, 0:1], rs5[:, c:c + 1], ALU.subtract,
                                      ALU.mult).then_inc(o_ready, 1)

            dve.wait_ge(parts_ready, JT)
            dve.wait_ge(x1_stored, JT)
            gat(0, None, 0)
            with dve.Fori(0, (NB1 - 1) // 2) as i:
                gat(2 * i + 1, 2 * i, 1)
                gat(2 * i + 2, 2 * i + 1, 0)
            for n in range(OUT_OPS):
                gat_out(NB1 - 1, n)
            gat_norm(NB1 - 1)


def kernel(**inputs):
    import numpy as _np
    import concourse.bacc as _bacc
    from concourse import mybir as _mybir
    from concourse.bass_utils import run_bass_kernel_spmd as _run

    v = {k: _np.asarray(a) for k, a in inputs.items()}
    adj = _np.zeros((NP, NP), _np.float32)
    adj[:N, :N] = v["adj"]
    x = _np.zeros((NP, H), _np.float32)
    x[:N] = v["x"]
    diag = _np.zeros((1, NP), _np.float32)
    diag[0, :N] = v["adj"].diagonal()
    sel = _np.zeros((19, 2, CNT + 1), _np.float32)
    for part in range(3):
        for h in range(HEADS):
            first, second = part * NV + 2 * h, part * NV + 2 * h + 1
            sel[first, 0, h] = sel[second, 1, h] = 1.0
            sel[first, 1, HEADS + h] = sel[second, 0, HEADS + h] = 1.0
    sel[18, 1, CNT] = 1.0
    gat_W, gat_a = v["L0_gnn_gat_W"], v["L0_gnn_gat_a"]
    W1, a1 = v["L1_gnn_W"], v["L1_gnn_a"]

    def bias(b):
        return b.reshape(6, P).T

    arrays = {
        "A": adj, "AT": adj.T, "x": x, "xT": x.T, "diag": diag,
        "W0": gat_W.transpose(1, 0, 2).reshape(H, HEADS * H),
        "W0T": gat_W.transpose(0, 2, 1).reshape(HEADS * H, H),
        "a0": gat_a.reshape(HEADS, 2, H).transpose(2, 0, 1),
        "eWi": v["L0_gnn_edge_Wih"].T, "eWh": v["L0_gnn_edge_Whh"].T,
        "ebi": bias(v["L0_gnn_edge_bih"]), "ebh": bias(v["L0_gnn_edge_bhh"]),
        "nWi": v["L0_gnn_node_Wih"].T, "nWh": v["L0_gnn_node_Whh"].T,
        "nbi": bias(v["L0_gnn_node_bih"]), "nbh": bias(v["L0_gnn_node_bhh"]),
        "W1": W1.transpose(1, 0, 2).reshape(H, H), "W1T": W1.transpose(2, 0, 1),
        "a1": a1.reshape(H1, 2, FO).transpose(2, 0, 1), "sel": sel,
    }
    arrays = {k: _np.ascontiguousarray(a) for k, a in arrays.items()}
    nc = _bacc.Bacc("TRN2", target_bir_lowering=False, num_devices=1)
    args = [nc.dram_tensor(f"in_{k}", a.shape, _mybir.dt.from_np(a.dtype), kind="ExternalInput").ap()
            for k, a in arrays.items()]
    out = nc.dram_tensor("out", (NP, H), _mybir.dt.float32, kind="ExternalOutput").ap()
    build(nc, *args, out)
    r = _run(nc, [{f"in_{k}": a for k, a in arrays.items()}], core_ids=[0])
    return r.results[0]["out"][:N]
```
